# Optimizing a Trainium2 kernel written in Bass

```python
import numpy as np
import jax
import jax.numpy as jnp

def _softmax(x, axis=-1):
    return jax.nn.softmax(x, axis=axis)

def _gelu(x):
    return jax.nn.gelu(x, approximate=True)

def _silu(x):
    return jax.nn.silu(x)

def _sigmoid(x):
    return jax.nn.sigmoid(x)

def _layernorm(x, axis=-1, eps=1e-05):
    m = jnp.mean(x, axis=axis, keepdims=True)
    v = jnp.var(x, axis=axis, keepdims=True)
    return (x - m) / jnp.sqrt(v + eps)

def _scatter_add(tgt, idx, src, axis=0):
    return tgt.at[idx].add(src)

def _segment_sum(src, seg, n):
    return jax.ops.segment_sum(src, seg, n)
kernel_name = 'mk_adaln_ffn_d2_seqx_r4_dd6d52'

def setup_inputs(seed: int=0):
    np.random.seed(seed)
    _w = jnp.asarray

    def _rec_inputs():
        import jax
        import jax.numpy as jnp
        _rk = jax.random.key(seed)
        x = -0.000125 + 0.9999 * jax.random.normal(jax.random.fold_in(_rk, 1), (128, 64, 1024), jnp.float32)
        _lenS = 64 - jax.random.randint(jax.random.fold_in(_rk, 7), (128,), 0, max(1, 64 // 4) + 1, jnp.int32)
        _lenS2 = 64 - jax.random.randint(jax.random.fold_in(_rk, 8), (128,), 0, max(1, 64 // 4) + 1, jnp.int32)
        cond_128 = 0.0061147 + 1.02565 * jax.random.normal(jax.random.fold_in(_rk, 11), (128, 128), jnp.float32)
        fside_S_0 = -0.022604 + 0.987366 * jax.random.normal(jax.random.fold_in(_rk, 12), (64,), jnp.float32)
        return (x, cond_128, fside_S_0)
    x, cond_128, fside_S_0 = _rec_inputs()

    def _L0_cond_setup():
        import jax, jax.numpy as jnp
        import numpy as np
        K = 8
        T = 1.0
        D_EMBD = 128
        IN_C = 64
        OUT_C = 64
        BS = 32
        H = 1024
        HID = 128
        key = jax.random.key(seed)
        ks = jax.random.split(key, 10)
        s = lambda fan_in: 1.0 / np.sqrt(fan_in)
        return {'x': jax.random.normal(ks[0], (BS, IN_C, H), dtype=jnp.float32), 'embedding': jax.random.normal(ks[1], (BS, D_EMBD), dtype=jnp.float32), 'W0': jax.random.normal(ks[2], (D_EMBD, HID), dtype=jnp.float32) * s(D_EMBD), 'b0': jnp.zeros((HID,), dtype=jnp.float32), 'W1': jax.random.normal(ks[3], (HID, HID), dtype=jnp.float32) * s(HID), 'b1': jnp.zeros((HID,), dtype=jnp.float32), 'W2': jax.random.normal(ks[4], (HID, K), dtype=jnp.float32) * s(HID), 'b2': jnp.zeros((K,), dtype=jnp.float32), 'weight': jax.random.normal(ks[5], (K, OUT_C, IN_C, 1), dtype=jnp.float32) * s(IN_C), 'bias_k': jax.random.normal(ks[6], (K, OUT_C), dtype=jnp.float32) * 0.1}
    _L0_cond_all = _L0_cond_setup()
    _L0_cond_in = {k: v for k, v in _L0_cond_all.items() if k in ('W0', 'b0', 'W1', 'b1', 'W2', 'b2', 'weight', 'bias_k')}
    del _L0_cond_all

    def _L0_ffn_setup():
        import jax, jax.numpy as jnp
        import numpy as np
        D_OUT, D_IN, RANK = (1024, 1024, 128)
        BATCH, SEQ = (4, 512)
        key = jax.random.key(seed)
        kx, ka, kb, kc = jax.random.split(key, 4)
        x = jax.random.normal(kx, (BATCH, SEQ, D_IN), dtype=jnp.float32)
        A = jax.random.normal(ka, (D_OUT, RANK), dtype=jnp.float32) * (1.0 / np.sqrt(RANK))
        B = jax.random.normal(kb, (D_IN, RANK), dtype=jnp.float32) * (1.0 / np.sqrt(D_IN))
        bias = jax.random.normal(kc, (D_OUT,), dtype=jnp.float32)
        return {'x': x, 'A': A, 'B': B, 'bias': bias}
    _L0_ffn_all = _L0_ffn_setup()
    _L0_ffn_in = {k: v for k, v in _L0_ffn_all.items() if k in ('A', 'B', 'bias')}
    del _L0_ffn_all

    def _L1_cond_setup():
        import jax, jax.numpy as jnp
        import numpy as np
        from jax import lax
        N, C_IN, L = (32, 64, 1024)
        C_OUT, K, GROUPS = (64, 9, 4)
        C_DIM, PAD, STRIDE = (128, 4, 1)
        key = jax.random.key(seed)
        k1, k2, k3, k4, k5 = jax.random.split(key, 5)
        x = jax.random.normal(k1, (N, C_IN, L), dtype=jnp.float32)
        c = jax.random.normal(k2, (N, C_DIM), dtype=jnp.float32)
        weight = jax.random.normal(k3, (C_OUT, C_IN // GROUPS, K), dtype=jnp.float32)
        c_weight = jax.random.normal(k4, (C_OUT, C_DIM), dtype=jnp.float32)
        bias = jax.random.normal(k5, (C_OUT,), dtype=jnp.float32)
        return {'x': x, 'c': c, 'weight': weight, 'c_weight': c_weight, 'bias': bias}
    _L1_cond_all = _L1_cond_setup()
    _L1_cond_in = {k: v for k, v in _L1_cond_all.items() if k in ('weight', 'c_weight')}
    del _L1_cond_all

    def _L1_ffn_setup():
        import jax, jax.numpy as jnp
        import numpy as np
        NUM_EXPERTS = 4
        HIDDEN = 1024
        RANK = 8
        ALPHA = 8.0
        SCALE = ALPHA / RANK
        key = jax.random.key(seed)
        ks = jax.random.split(key, 6)
        B, T, H, E, R = (4, 1024, HIDDEN, NUM_EXPERTS, RANK)
        x = jax.random.normal(ks[0], (B, T, H), dtype=jnp.float32)
        W_up = jax.random.normal(ks[1], (H, H), dtype=jnp.float32) / np.sqrt(H)
        gate_w = jax.random.normal(ks[2], (E, H), dtype=jnp.float32) / np.sqrt(H)
        expert_bias = jnp.zeros((E,), dtype=jnp.float32)
        lora_A = jax.random.normal(ks[3], (E, R, H), dtype=jnp.float32) / np.sqrt(H)
        lora_B = jax.random.normal(ks[4], (E, H, R), dtype=jnp.float32) * 0.01
        return {'x': x, 'W_up': W_up, 'gate_w': gate_w, 'expert_bias': expert_bias, 'lora_A': lora_A, 'lora_B': lora_B}
    _L1_ffn_all = _L1_ffn_setup()
    _L1_ffn_in = {k: v for k, v in _L1_ffn_all.items() if k in ('W_up', 'gate_w', 'expert_bias', 'lora_A', 'lora_B')}
    del _L1_ffn_all
    return {'x': x, 'cond_128': cond_128, 'fside_S_0': fside_S_0, 'L0_cond_W0': _L0_cond_in['W0'], 'L0_cond_b0': _L0_cond_in['b0'], 'L0_cond_W1': _L0_cond_in['W1'], 'L0_cond_b1': _L0_cond_in['b1'], 'L0_cond_W2': _L0_cond_in['W2'], 'L0_cond_b2': _L0_cond_in['b2'], 'L0_cond_weight': _L0_cond_in['weight'], 'L0_cond_bias_k': _L0_cond_in['bias_k'], 'L0_ffn_A': _L0_ffn_in['A'], 'L0_ffn_B': _L0_ffn_in['B'], 'L0_ffn_bias': _L0_ffn_in['bias'], 'L1_cond_weight': _L1_cond_in['weight'], 'L1_cond_c_weight': _L1_cond_in['c_weight'], 'L1_ffn_W_up': _L1_ffn_in['W_up'], 'L1_ffn_gate_w': _L1_ffn_in['gate_w'], 'L1_ffn_expert_bias': _L1_ffn_in['expert_bias'], 'L1_ffn_lora_A': _L1_ffn_in['lora_A'], 'L1_ffn_lora_B': _L1_ffn_in['lora_B']}

def reference(x, cond_128, fside_S_0, L0_cond_W0, L0_cond_b0, L0_cond_W1, L0_cond_b1, L0_cond_W2, L0_cond_b2, L0_cond_weight, L0_cond_bias_k, L0_ffn_A, L0_ffn_B, L0_ffn_bias, L1_cond_weight, L1_cond_c_weight, L1_ffn_W_up, L1_ffn_gate_w, L1_ffn_expert_bias, L1_ffn_lora_A, L1_ffn_lora_B):
    import jax
    import jax.numpy as jnp

    def _L0_cond_ref(x, embedding, W0, b0, W1, b1, W2, b2, weight, bias_k):
        import jax, jax.numpy as jnp
        import numpy as np
        K = 8
        T = 1.0
        D_EMBD = 128
        IN_C = 64
        OUT_C = 64
        BS = 32
        H = 1024
        HID = 128
        h = jax.nn.gelu(embedding @ W0 + b0, approximate=False)
        h = jax.nn.gelu(h @ W1 + b1, approximate=False)
        att = jax.nn.softmax((h @ W2 + b2) / T, axis=-1)
        agg_w = jnp.einsum('bk,koi->boi', att, weight[..., 0])
        agg_b = att @ bias_k
        out = jnp.einsum('boi,bih->boh', agg_w, x) + agg_b[:, :, None]
        return out

    def _L0_ffn_ref(x, A, B, bias):
        import jax, jax.numpy as jnp
        import numpy as np
        D_OUT, D_IN, RANK = (1024, 1024, 128)
        BATCH, SEQ = (4, 512)
        weight = A @ B.T
        out = jnp.einsum('bsd,od->bso', x, weight) + bias
        return out

    def _L1_cond_ref(x, c, weight, c_weight, bias):
        import jax, jax.numpy as jnp
        import numpy as np
        from jax import lax
        N, C_IN, L = (32, 64, 1024)
        C_OUT, K, GROUPS = (64, 9, 4)
        C_DIM, PAD, STRIDE = (128, 4, 1)
        out = lax.conv_general_dilated(x, weight, window_strides=(STRIDE,), padding=[(PAD, PAD)], dimension_numbers=('NCH', 'OIH', 'NCH'), feature_group_count=GROUPS)
        ctx = jnp.einsum('nd,od->no', c, c_weight)
        out = out + ctx[:, :, None] + bias[None, :, None]
        return out

    def _L1_ffn_ref(x, W_up, gate_w, expert_bias, lora_A, lora_B):
        import jax, jax.numpy as jnp
        import numpy as np
        NUM_EXPERTS = 4
        HIDDEN = 1024
        RANK = 8
        ALPHA = 8.0
        SCALE = ALPHA / RANK
        B, T, H = x.shape
        E = gate_w.shape[0]
        x_flat = x.reshape(-1, H)
        logits = x_flat @ gate_w.T + expert_bias
        top1 = jnp.argmax(logits, axis=-1)
        one_hot = jax.nn.one_hot(top1, E, dtype=x_flat.dtype)
        base_out = jnp.einsum('bth,oh->bto', x, W_up)
        z = jnp.einsum('nh,erh->ner', x_flat, lora_A)
        d = jnp.einsum('ner,ehr->neh', z, lora_B) * SCALE
        delta = jnp.einsum('neh,ne->nh', d, one_hot)
        return base_out + delta.reshape(B, T, H)
    x = x + _L0_ffn_ref(_L0_cond_ref(x, cond_128, L0_cond_W0, L0_cond_b0, L0_cond_W1, L0_cond_b1, L0_cond_W2, L0_cond_b2, L0_cond_weight, L0_cond_bias_k), L0_ffn_A, L0_ffn_B, L0_ffn_bias)
    x = x + _L1_ffn_ref(_L1_cond_ref(x, cond_128, L1_cond_weight, L1_cond_c_weight, fside_S_0), L1_ffn_W_up, L1_ffn_gate_w, L1_ffn_expert_bias, L1_ffn_lora_A, L1_ffn_lora_B)
    return x

_drawn_inputs = setup_inputs


def setup_inputs(seed=0):
    import zlib

    import numpy as np

    out = dict(_drawn_inputs(seed))
    spreads = {'L0_cond_b0': (0.0, 0.8),
     'L0_cond_b1': (0.0, 0.55),
     'L0_cond_b2': (0.0, 0.526),
     'L1_ffn_expert_bias': (0.0, 0.8)}
    factors = {'L0_cond_bias_k': 2.669}
    for name, (base, spread) in spreads.items():
        noise = np.random.default_rng([zlib.crc32(name.encode()), seed]).standard_normal(out[name].shape)
        drawn = base * np.exp(spread * noise) if base else spread * noise
        out[name] = jnp.asarray(drawn.astype(out[name].dtype))
    for name, factor in factors.items():
        out[name] = (out[name] * factor).astype(out[name].dtype)
    return out
```

```python
import concourse.bass as bass
from concourse import mybir
from contextlib import ExitStack

NB = 128
C = 64
L = 1024
RK = 128
E = 4
R = 8
NG = 4
NS = 32
WC = 36 + L
CH = [(0, 380), (380, 344), (724, 336)]
OFF = [36, 0, 0]
NA = [43, 43, 42]
A0 = [0, 43, 86]
XR = 5
YR = 3


def adaln_ffn(nc, x, cond, fside, W0, b0, W1, b1, W2, b2, wk, bias_k, A, B, fbias,
              cw, ccw, Wup, gate, ebias, loA, loB, out):
    fp32 = mybir.dt.float32
    f32r = mybir.dt.float32r
    ALU = mybir.AluOpType
    ACT = mybir.ActivationFunctionType
    AX = mybir.AxisListType

    x_v = x.rearrange("b c l -> (b c) l").rearrange("(s q p) l -> s p q l", q=2, p=128)
    out_v = out.rearrange("b c l -> (b c) l").rearrange("(t p) l -> t p l", p=128)
    aggD = nc.dram_tensor("agg_scratch", (NB, C, C), fp32, kind="Internal").ap()
    agbD = nc.dram_tensor("agb_scratch", (NB, C), fp32, kind="Internal").ap()
    tapD = nc.dram_tensor("tap_scratch", (C, 16, 24), fp32, kind="Internal").ap()

    ctx = ExitStack()
    with ctx:
        place = {"": (nc.sbuf_base + 31) // 32 * 32}

        def sb(name, shape, dt=fp32):
            size = 4
            for n in shape[1:]:
                size *= n
            place[name] = place[""]
            place[""] += (size + 31) // 32 * 32
            assert place[""] <= nc.sbuf_usable_end
            return nc.alloc_sbuf_tensor_at(name, shape, dt, offset=place[name])

        def over(name, base, shape, start=0):
            return nc.alloc_sbuf_tensor_at(name, shape, fp32, offset=place[base] + 4 * start)

        Wh = sb("Wh", [128, 8, WC], f32r)
        Wl = sb("Wl", [128, 8, WC], f32r)
        Ah = sb("Ah", [128, 8, 128], f32r)
        Al = sb("Al", [128, 8, 128], f32r)
        Bh = sb("Bh", [128, 8, RK], f32r)
        Bl = sb("Bl", [128, 8, RK], f32r)
        Th = sb("Th", [128, NG, 2, 8, 16], f32r)
        Tl = sb("Tl", [128, NG, 2, 8, 16], f32r)
        Ls = sb("Ls", [96, L], f32r)
        biasb = sb("biasb", [128, L])
        ident = sb("ident", [128, 128])
        cb = sb("cb", [128, NB, NG])
        csB = sb("csB", [128, 1])
        ebb = sb("ebb", [128, E])
        wts = sb("wts", [128, E])
        xin = sb("xin", [128, 2, L])
        xTh = sb("xTh", [128, 8, 256], f32r)
        xTl = sb("xTl", [128, 8, 256], f32r)
        D = over("D", "xTh", [128, NG, 512])
        uT = sb("uT", [128, 256])
        u = sb("u", [128, 256])
        agg = sb("agg", [128, 2, 128])
        agb = sb("agb", [128, 256])
        v = sb("v", [128, 256])
        vh = sb("vh", [128, 256], f32r)
        vl = sb("vl", [128, 256], f32r)
        x1 = sb("x1", [128, XR, 8, 129])
        Xlo = sb("Xlo", [128, 4, NG, 129], f32r)
        Xhi = sb("Xhi", [128, 4, NG, 129], f32r)
        yh = sb("yh", [128, YR, 8, 128], f32r)
        yl = sb("yl", [128, YR, 8, 128], f32r)
        osb = sb("osb", [128, L])
        lg = sb("lg", [128, E])
        mx = sb("mx", [128, 1])
        sc = sb("sc", [128, E])
        m2 = sb("m2", [128, 1])
        zm = sb("zm", [128, E * R])
        zs = sb("zs", [128, 96])
        zst = sb("zst", [96, 128], f32r)

        O = [ctx.enter_context(nc.psum_tensor(f"O{i}", [128, 512], fp32)) for i in range(3)]
        F = [ctx.enter_context(nc.psum_tensor(f"F{i}", [128, 512], fp32)) for i in range(5)]
        P = O + F

        queues = {e: [] for e in ("pe", "act", "dve", "pool", "sp")}
        sems, counts = {}, {}

        def do(engine, emit, after=(), sem=None, by=1):
            queues[engine].append((emit, [a for a in after if a], sem, by))
            if sem is None:
                return None
            if sem not in sems:
                sems[sem] = ctx.enter_context(nc.semaphore(sem))
                counts[sem] = 0
            counts[sem] += by
            return sem, counts[sem]

        def play(engine, eng):
            known = {}
            for emit, after, sem, by in queues[engine]:
                for name, value in after:
                    if known.get(name, 0) < value:
                        eng.wait_ge(sems[name], value)
                        known[name] = value
                ins = emit(eng)
                if sem is not None:
                    ins.then_inc(sems[sem], by)

        def load(dst, src, after=(), sem="d_set"):
            return do("sp", lambda e: e.dma_start(dst, src), after, sem, 16)

        def seq(*emits):
            def go(e):
                for f in emits:
                    last = f(e)
                return last
            return go

        def flat(t, n):
            return t[:, :, :].bitcast(fp32).rearrange("p a b -> p (a b)")[:, 0:n]

        xflat = xin[:, :, :].rearrange("p a b -> p (a b)")
        cnd = xflat[:, 0:128]
        W0s = xflat[:, 128:256]
        W1s = xflat[:, 256:384]
        W2s = xflat[:, 384:392]
        b2s = xflat[:, 392:400]
        b0s = xflat[:, 400:401]
        b1s = xflat[:, 401:402]
        fsc = xflat[:, 404:408]
        cwn = xflat[0:64, 512:640]
        bks = xflat[0:8, 640:704]
        condT = xflat[:, 768:896]
        h1 = xflat[:, 896:1024]
        h2 = xflat[:, 1024:1152]
        att = xflat[:, 1152:1160]
        atn = xflat[:, 1160:1168]
        nmx = xflat[:, 1168:1169]
        ssum = xflat[:, 1169:1170]
        rs = xflat[:, 1170:1171]
        ones = xflat[:, 1171:1172]
        attT = xflat[0:8, 1184:1312]
        ccT = xflat[:, 1312:1376]
        agbs = xflat[:, 1408:1472]
        wks = x1[:, :, :, :].rearrange("p a b c -> p (a b c)")[0:8, 0:4096]
        aggS = over("aggS", "yh", [128, C, 32])
        aggS2 = over("aggS2", "yl", [128, C, 32])
        taps = over("taps", "xTl", [64, 16, 24])
        tapn = over("tapn", "xTl", [64, 16, 9], 384)
        cwX = over("cwX", "xTl", [128, NG, 8, 16], 1024)
        Uw = over("Uw", "xTh", [128, C, 16])
        Braw = over("Braw", "Xlo", [128, 8, RK])
        Araw = over("Araw", "Xlo", [128, 8, RK], 1024)
        LBr = over("LBr", "Xhi", [128, 8, E, R])
        LB3 = over("LB3", "Xhi", [128, 8, 3, E * R], 256)
        Graw = over("Graw", "Xhi", [36, L], 1024)

        do("pool", lambda e: e.memset(ident[:, :], 0.0), sem="g_id")
        d_id = do("pool", lambda e: e.affine_select(out=ident[:, :], in_=ident[:, :], compare_op=ALU.not_equal,
                                                    fill=1.0, base=0, pattern=[[-1, 128]], channel_multiplier=1),
                  [("g_id", 1)], "g_id")
        for i in range(E):
            do("pool", lambda e, i=i: e.memset(wts[:, i:i + 1], float(E - i)))
        do("pool", lambda e: e.memset(agg[:, :, :], 0.0), sem="g_agg0")
        d_on = do("pool", lambda e: e.memset(ones, 1.0), sem="g_id")
        d_tap0 = do("pool", lambda e: e.memset(taps[:, :, :], 0.0), sem="g_id")

        lc = load(cnd, cond, sem="d_cnd")
        load(W0s, W0, sem="d_mlp")
        load(b0s, b0.rearrange("(p a) -> p a", a=1), sem="d_mlp")
        load(W1s, W1, sem="d_mlp")
        load(b1s, b1.rearrange("(p a) -> p a", a=1), sem="d_mlp")
        load(W2s, W2, sem="d_mlp")
        lm = load(b2s, b2.rearrange("(a k) -> a k", a=1).broadcast_to([128, 8]), sem="d_mlp")
        lt = load(tapn[:, :, :], cw, sem="d_tap")
        load(Braw[:, :, :], B.rearrange("(j c) k -> j c k", c=8), sem="d_ab")
        lab = load(Araw[:, :, :], A.rearrange("(j c) k -> j c k", c=8), sem="d_ab")
        load(wks, wk.rearrange("k o i a -> k (o i a)"), sem="d_wk")
        lk = load(bks, bias_k, sem="d_wk")
        load(cwn, ccw, sem="d_cc")
        for r in range(8):
            lcc = do("sp", lambda e, r=r: e.dma_start(fsc[16 * r:16 * r + 16, :], fside.rearrange("(g o) -> o g", o=16), allow_slow_non_contiguous=True), (), "d_cc", 16)
        load(biasb[:, :], fbias.rearrange("(a n) -> a n", a=1).broadcast_to([128, L]), sem="d_lo")
        load(ebb[:, :], ebias.rearrange("(a n) -> a n", a=1).broadcast_to([128, E]), sem="d_lo")
        load(Graw[0:4, :], gate, sem="d_lo")
        load(Graw[4:36, :], loA.rearrange("e r h -> (e r) h"), sem="d_lo")
        for e_ in range(E):
            llo = load(LBr[:, :, e_, :], loB[e_].rearrange("(m p) r -> p m r", p=128), sem="d_lo")

        for k in range(9):
            vt = do("dve", lambda e, k=k: e.tensor_copy(taps[:, :, 15 - k:16 - k], tapn[:, :, k:k + 1]),
                    [lt, d_tap0], "v_tap")
        st = do("sp", lambda e: e.dma_start(tapD, taps[:, :, :]), [vt], "d_tapw", 16)
        for r in range(8):
            lu = load(Uw[r::8, :, :], tapD[:, :, 7 - r:23 - r].rearrange("o i m -> i o m"), [st], "d_tapr")
        for blk in range(2):
            src = Uw[:, :, 8 - 8 * blk:16 - 8 * blk].rearrange("p (g o) r -> p g r o", g=NG)
            t_h = [do("dve", lambda e, g=g, blk=blk, src=src: e.tensor_copy(Th[:, g, blk], src[:, g]), [lu], "v_set")
                   for g in range(NG)]
            for g in range(NG):
                t_set = do("dve", lambda e, g=g, blk=blk, src=src: e.tensor_tensor(
                    Tl[:, g, blk], src[:, g], Th[:, g, blk].bitcast(fp32), ALU.subtract), [t_h[g]], "v_set")

        pc = do("pe", lambda e: e.transpose(F[4][:, 0:128], cnd, ident[:, :]), [lc, d_id], "p_set")
        ac = do("act", lambda e: e.activation(condT, F[4][:, 0:128], ACT.Copy), [pc], "a_set")
        p1 = do("pe", lambda e: e.matmul(F[4][:, 128:256], W0s, condT, start=True, stop=True), [ac, lm], "p_set")
        a1 = do("act", lambda e: e.activation(h1, F[4][:, 128:256], ACT.Gelu, bias=b0s), [p1], "a_set")
        p2 = do("pe", lambda e: e.matmul(F[4][:, 256:384], W1s, h1, start=True, stop=True), [a1], "p_set")
        a2 = do("act", lambda e: e.activation(h2, F[4][:, 256:384], ACT.Gelu, bias=b1s), [p2], "a_set")
        p3 = do("pe", lambda e: e.matmul(F[4][:, 384:392], h2, W2s, start=True, stop=True), [a2], "p_set")
        w1 = do("dve", lambda e: e.tensor_tensor(att, F[4][:, 384:392], b2s, ALU.add), [p3, lm], "v_set")
        w2 = do("dve", lambda e: e.tensor_reduce(nmx, att, AX.X, ALU.max, negate=True), [w1], "v_set")
        a3 = do("act", lambda e: e.activation(atn, att, ACT.Exp, bias=nmx, accum_out=ssum), [w2], "a_set")
        w3 = do("dve", lambda e: e.reciprocal(rs, ssum), [a3], "v_set")
        w4 = do("dve", lambda e: e.tensor_scalar(att, atn, rs, None, ALU.mult), [w3, a3], "v_set")
        p4 = do("pe", lambda e: e.transpose(F[3][0:8, 0:128], att, ident[:, :]), [w4], "p_set")
        w5 = do("dve", lambda e: e.tensor_copy(attT, F[3][0:8, 0:128]), [p4], "v_set")
        last = [None] * 8
        for c in range(8):
            pg = do("pe", lambda e, c=c: e.matmul(P[c % 4][:, :], attT, wks[:, 512 * c:512 * c + 512],
                                                  start=True, stop=True), [w5, lk, last[c - 4] if c >= 4 else None], "p_set")
            dst = (aggS, aggS2)[c // 4][:, :, 8 * (c % 4):8 * (c % 4) + 8]
            last[c] = do("dve", lambda e, c=c, dst=dst: e.tensor_copy(
                dst.rearrange("p i o -> p o i"), P[c % 4][:, :].rearrange("p (o i) -> p o i", o=8)), [pg], "v_set")
        pb = do("pe", lambda e: e.matmul(F[4][:, 0:64], attT, bks, start=True, stop=True), [w5, lk], "p_set")
        vb = do("dve", lambda e: e.tensor_copy(agbs, F[4][:, 0:64]), [pb], "v_set")
        for h in range(2):
            do("sp", lambda e, h=h: e.dma_start(aggD[:, :, 32 * h:32 * h + 32],
                                                (aggS, aggS2)[h][:, :, :]), [last[4 * h + 3]], "d_agw", 16)
        d_agw = do("sp", lambda e: e.dma_start(agbD, agbs), [vb], "d_agw", 16)

        b_h = do("act", lambda e: e.activation(Bh[:, :, :], Braw[:, :, :], ACT.Copy), [lab], "a_set")
        b_l = do("dve", lambda e: e.tensor_tensor(Bl[:, :, :], Braw[:, :, :], Bh[:, :, :].bitcast(fp32), ALU.subtract), [b_h], "v_set")
        pcs = do("pe", seq(*[lambda e, c=c: e.matmul(F[3][:, 0:1], Braw[:, c, :], ones, start=c == 0, stop=c == 7)
                             for c in range(8)]), [lab, d_on, w5], "p_set")
        csb = do("dve", lambda e: e.tensor_copy(csB[:, :], F[3][:, 0:1]), [pcs], "v_set")
        for h in range(2):
            pa = do("pe", seq(*[lambda e, h=h, c=c: e.transpose(F[h][:, 128 * c:128 * c + 128], Araw[:, 4 * h + c, :], ident[:, :])
                                for c in range(4)]), [lab, last[7], d_id], "p_set")
            ah = do("act", lambda e, h=h: e.activation(Ah[:, 4 * h:4 * h + 4, :].rearrange("p a b -> p (a b)"), F[h][:, :], ACT.Copy),
                    [pa], "a_set")
            al = do("dve", lambda e, h=h: e.tensor_tensor(Al[:, 4 * h:4 * h + 4, :].rearrange("p a b -> p (a b)"), F[h][:, :],
                                                          Ah[:, 4 * h:4 * h + 4, :].rearrange("p a b -> p (a b)").bitcast(fp32),
                                                          ALU.subtract), [ah], "v_set")
        pcc = do("pe", lambda e: e.transpose(F[4][:, 64:128], cwn, ident[0:64, 0:64]), [lcc, vb], "p_set")
        acc = do("dve", lambda e: e.tensor_copy(ccT, F[4][:, 64:128]), [pcc], "v_set")
        for g in range(NG):
            vx = do("dve", lambda e, g=g: e.tensor_copy(cwX[:, g], ccT[:, 16 * g:16 * g + 16].unsqueeze(1).broadcast_to([128, 8, 16])),
                    [acc], "v_set")
        for g in range(NG):
            pcb = do("pe", lambda e, g=g: e.matmul(F[2][:, 128 * g:128 * g + 128], cwX[:, g].rearrange("p r o -> p (r o)"), condT,
                                                   start=True, stop=True), [vx, ac], "p_set")
        for g in range(NG):
            vcb = do("dve", lambda e, g=g: e.tensor_scalar(cb[:, :, g], F[2][:, 128 * g:128 * g + 128], fsc[:, g:g + 1], None, ALU.add),
                     [pcb, lcc], "v_set")
        LB2 = LBr[:, :, :, :].rearrange("p m e r -> p m (e r)")
        for t in range(2):
            l_h = do("dve", lambda e, t=t: e.tensor_copy(LB3[:, :, t, :].bitcast(f32r), LB2), [llo], "v_set")
        l_l = do("dve", lambda e: e.tensor_tensor(LB3[:, :, 2, :].bitcast(f32r), LB2, LB3[:, :, 0, :], ALU.subtract), [l_h], "v_set")
        for h in range(2):
            pl = do("pe", seq(*[lambda e, h=h, m=m: e.transpose(F[h][0:96, 128 * m:128 * m + 128],
                                                               LB3[:, 4 * h + m].rearrange("p t n -> p (t n)"), ident[:, :])
                                for m in range(4)]), [l_l, al], "p_set")
            l_s = do("act", lambda e, h=h: e.activation(Ls[:, 512 * h:512 * h + 512], F[h][0:96, :], ACT.Copy), [pl], "a_set")
        pg = do("pe", seq(*[lambda e, c=c: e.transpose(F[3][:, 36 * c:36 * c + 36], Graw[:, c::8], ident[0:36, 0:36])
                            for c in range(8)]), [llo, csb], "p_set")
        gh = do("act", lambda e: e.activation(Wh[:, :, 0:36], F[3][:, 0:288].rearrange("p (c n) -> p c n", c=8), ACT.Copy), [pg], "a_set")
        gl = do("dve", lambda e: e.tensor_tensor(Wl[:, :, 0:36], F[3][:, 0:288].rearrange("p (c n) -> p c n", c=8),
                                                 Wh[:, :, 0:36].bitcast(fp32), ALU.subtract), [gh], "v_set")
        x1f = x1[:, :, :, :].rearrange("p a b c -> p (a b c)")
        yhf = over("yhf", "yh", [128, YR * L])
        ylf = over("ylf", "yl", [128, YR * L])
        stage = [x1f[:, 0:1024], x1f[:, 1024:2048], x1f[:, 2048:3072], x1f[:, 3072:4096],
                 yhf[:, 2048:3072], ylf[:, 2048:3072], yhf[:, 0:1024], ylf[:, 0:1024]]
        after = [[last[7], pg]] * 4 + [[], []] + [[("d_agw", 48)]] * 2
        rel = {}
        wl = [None, None]
        for m in range(8):
            wl[m // 4] = load(stage[m], Wup[128 * m:128 * m + 128, :], after[m], f"d_wup{m // 4}")
        n = 0
        w_done = None
        for half in range(2):
            for c in range(8):
                bank = P[n % 8]
                pre = [wl[half], d_id, rel.get(n - 8)] + ([l_s, vcb, gl, csb, vb, l_l, al] if n == 0 else [])
                pw = do("pe", seq(*[lambda e, m=m, c=c, bank=bank, half=half: e.transpose(
                    bank[:, 128 * m:128 * m + 128], stage[4 * half + m][:, c::8], ident[:, :]) for m in range(4)]), pre, "p_w")
                lo, hi = 36 + 512 * half, 36 + 512 * half + 512
                aw = do("act", lambda e, bank=bank, c=c, lo=lo, hi=hi: e.activation(Wh[:, c, lo:hi], bank[:, :], ACT.Copy), [pw], "a_w")
                rel[n] = w_done = do("dve", lambda e, bank=bank, c=c, lo=lo, hi=hi: e.tensor_tensor(
                    Wl[:, c, lo:hi], bank[:, :], Wh[:, c, lo:hi].bitcast(fp32), ALU.subtract), [aw], "v_w")
                n += 1
        zp1 = do("pool", lambda e: e.memset(x1[:, :, 0:4, 0:1], 0.0), [pw], "g_set")
        zp2 = do("pool", lambda e: e.memset(x1[:, :, 4:8, 128:129], 0.0), [pw], "g_set")

        T = {}

        def g_(key):
            return T.get(key)

        def load_x(s):
            T["x", s] = do("sp", lambda e: e.dma_start(xin[:, :, :], x_v[s]),
                           [g_(("xb", s - 1, 1)), g_(("tx", s - 1, 3))] + ([pg, vcb, pcb, w_done, ("d_agw", 48)] if s == 0 else []), "d_x", 16)

        def load_ag(s):
            prev = [g_(("v", s - 1)), g_(("vv", s - 1))] + ([("d_agw", 48), ("g_agg0", 1)] if s == 0 else [])
            for b in range(2):
                src = aggD[4 * s + b:4 * s + b + 3:2].rearrange("q c o -> c q o")
                do("sp", lambda e, b=b, src=src: e.dma_start(agg[64 * b:64 * b + 64, :, 64 * b:64 * b + 64], src), prev, "d_ag", 16)
            src = agbD[4 * s:4 * s + 4, :].rearrange("(a b) o -> a (b o)", a=1).broadcast_to([128, 256])
            T["ag", s] = do("sp", lambda e: e.dma_start(agb[:, :], src), prev, "d_ag", 16)

        def unit_tx(s, i):
            q, h = i // 2, i % 2
            T["tx", s, i] = do("pe", seq(*[lambda e, c=c: e.transpose(F[i][:, 128 * c:128 * c + 128], xin[:, q, 4 * h + c::8], ident[:, :])
                                           for c in range(4)]), [T["x", s], g_(("yl", s - 2, i)), g_(("x1", s - 1, i)), w_done], "p_tx")
            dh = xTh[:, 4 * h:4 * h + 4, 128 * q:128 * q + 128]
            dl = xTl[:, 4 * h:4 * h + 4, 128 * q:128 * q + 128]
            src = F[i][:, :].rearrange("p (c t) -> p c t", c=4)
            T["txh", s, i] = do("act", lambda e: e.activation(dh, src, ACT.Copy),
                                [T["tx", s, i], g_(("td", s - 2, 3)), g_(("u", s - 1)), t_set], "a_txh")
            T["txl", s, i] = do("dve", lambda e: e.tensor_tensor(dl, src, dh.bitcast(fp32), ALU.subtract),
                                [T["txh", s, i], g_(("u", s - 1))], "v_txl")

        def unit_u(s, half):
            ms = []
            for c in range(4 * half, 4 * half + 4):
                for n_, (w, m) in enumerate(((Bh, xTh), (Bh, xTl), (Bl, xTh))):
                    ms.append(lambda e, c=c, w=w, m=m, n_=n_: e.matmul(F[4][:, 0:256], w[:, c, :], m[:, c, :],
                                                                      start=c == 0 and n_ == 0, stop=c == 7 and n_ == 2))
            T["u", s] = do("pe", seq(*ms), [T["txl", s, 3], g_(("vv", s - 1)), b_h, b_l], "p_u")
            if half:
                T["ut", s] = do("act", lambda e: e.activation(uT[:, :], F[4][:, 0:256], ACT.Copy), [T["u", s], g_(("tu", s - 1))], "a_u")

        def unit_tu(s):
            T["tu", s] = do("pe", seq(*[lambda e, q=q: e.transpose(F[4][:, 128 * q:128 * q + 128], uT[:, 128 * q:128 * q + 128], ident[:, :])
                                        for q in range(2)]), [T["ut", s]], "p_tu")
            T["tuu", s] = do("act", lambda e: e.activation(u[:, :], F[4][:, 0:256], ACT.Copy), [T["tu", s], g_(("v", s - 1))], "a_tu")

        def unit_v(s):
            T["v", s] = do("pe", seq(*[lambda e, q=q: e.matmul(F[4][:, 128 * q:128 * q + 128], u[:, 128 * q:128 * q + 128], agg[:, q, :],
                                                               start=True, stop=True) for q in range(2)]),
                           [T["tuu", s], T["ag", s]], "p_v")
            T["vv", s] = do("dve", lambda e: e.scalar_tensor_tensor(out=v[:, :], in0=agb[:, :], scalar=csB[:, 0:1], in1=F[4][:, 0:256],
                                                                    op0=ALU.mult, op1=ALU.add),
                            [T["v", s], T["ag", s], g_(("vh", s - 1)), csb, g_(("vl", s - 1))], "v_v")
            T["vh", s] = do("act", lambda e: e.activation(vh[:, :], v[:, :], ACT.Copy), [T["vv", s], g_(("o", s - 1, 3))], "a_vh")
            T["vl", s] = do("dve", lambda e: e.tensor_tensor(vl[:, :], v[:, :], vh[:, :].bitcast(fp32), ALU.subtract),
                            [T["vh", s], g_(("o", s - 1, 3))], "v_vl")

        def slot(s, q):
            return (2 * s + q) % XR

        def unit_xb(s, q):
            t = 2 * s + q
            xs = xin[:, q, :].rearrange("p (a c) -> p c a", c=8)
            bs = biasb[:, :].rearrange("p (a c) -> p c a", c=8)
            o = x1[:, slot(s, q)]
            for h in range(2):
                dst = o[:, 4:8, 0:128] if h == 0 else o[:, 0:4, 1:129]
                T["xb", s, q] = do("pool", lambda e, h=h, dst=dst: e.tensor_tensor(dst, xs[:, 4 * h:4 * h + 4, :], bs[:, 4 * h:4 * h + 4, :], ALU.add),
                                   [T["x", s], g_(("f", t - XR, 2)), g_(("rx", (t - XR) // 2, (t - XR) % 2)), zp1, zp2, llo], "g_xb")

        def unit_o(s, i):
            q, h = i // 2, i % 2
            ms = []
            for n_, (w, m) in enumerate(((vh, Ah), (vh, Al), (vl, Ah))):
                ms.append(lambda e, w=w, m=m, n_=n_: e.matmul(F[i][:, :], w[:, 128 * q:128 * q + 128],
                                                             m[:, 4 * h:4 * h + 4, :].rearrange("p c a -> p (c a)"),
                                                             start=n_ == 0, stop=n_ == 2))
            T["o", s, i] = do("pe", seq(*ms), [T["vl", s], g_(("txl", s, i)), g_(("dd", s - 1, i)), ah, al], "p_o")
            o = x1[:, slot(s, q)]
            dst = o[:, 4:8, 0:128] if h == 0 else o[:, 0:4, 1:129]
            T["x1", s, i] = do("dve", lambda e: e.tensor_tensor(dst, F[i][:, :].rearrange("p (c a) -> p c a", c=4), dst, ALU.add),
                               [T["o", s, i], T["xb", s, q]], "v_x1")
            if h:
                for b in range(2):
                    for g in range(NG):
                        p0 = 64 * b + 16 * g
                        T["rx", s, q] = do("sp", lambda e, b=b, g=g, p0=p0: e.dma_start(
                            Xlo[:, 2 * q + b, g, :].bitcast(fp32), x1[p0:p0 + 16, slot(s, q), :, :]),
                            [T["x1", s, i], g_(("c", s - 1, 3)), b_l, pa], "d_rx", 16)

        def unit_xs(s):
            T["xs1", s] = do("act", lambda e: e.activation(Xhi[:, :, :, :], Xlo[:, :, :, :].bitcast(fp32), ACT.Copy),
                             [T["rx", s, 1], g_(("c", s - 1, 3)), pl, pg], "a_xs")
            T["xs", s] = do("dve", lambda e: e.tensor_tensor(Xlo[:, :, :, :], Xlo[:, :, :, :].bitcast(fp32),
                                                            Xhi[:, :, :, :].bitcast(fp32), ALU.subtract), [T["xs1", s]], "v_xs")

        def unit_c(s, g):
            ms = []
            for blk in range(2):
                for n_, (w, m) in enumerate(((Th, Xhi), (Tl, Xhi), (Th, Xlo))):
                    ms.append(lambda e, w=w, m=m, blk=blk, n_=n_: e.matmul(
                        F[g][:, :], w[:, g, blk].rearrange("p r o -> p (r o)"), m[:, :, g, blk:blk + 128],
                        start=blk == 0 and n_ == 0, stop=blk == 1 and n_ == 2))
            T["c", s, g] = do("pe", seq(*ms), [T["xs", s], g_(("txl", s + 1, g)), g_(("x1", s, g)), t_set], "p_c")
            T["dd", s, g] = do("dve", lambda e: e.tensor_tensor(
                D[:, g, :].rearrange("p (b j) -> p b j", b=4), F[g][:, :].rearrange("p (b j) -> p b j", b=4),
                cb[:, 4 * s:4 * s + 4, g].unsqueeze(2).broadcast_to([128, 4, 128]), ALU.add),
                [T["c", s, g], g_(("u", s + 1)), g_(("td", s - 1, 3)), vcb], "v_d")

        def unit_td(s, b):
            q, bb = b // 2, b % 2
            ys = (2 * s + q) % YR
            T["td", s, b] = do("pe", seq(*[lambda e, g=g: e.transpose(F[b][:, 128 * g:128 * g + 128], D[:, g, 128 * b:128 * b + 128], ident[:, :])
                                           for g in range(NG)]), [T["dd", s, 3], g_(("x1", s + 1, b))], "p_td")
            src = F[b][:, :].rearrange("p (g r o) -> p r g o", g=NG, r=8)
            dh = yh[:, ys, :, 64 * bb:64 * bb + 64].rearrange("p r (g o) -> p r g o", g=NG)
            dl = yl[:, ys, :, 64 * bb:64 * bb + 64].rearrange("p r (g o) -> p r g o", g=NG)
            pt = 2 * s + q - YR
            wait = [T["td", s, b], g_(("cc", pt, 2)), pw, ("d_agw", 48)]
            T["yh", s, b] = do("act", lambda e: e.activation(dh, src, ACT.Copy), wait, "a_yh")
            T["yl", s, b] = do("dve", lambda e: e.tensor_tensor(dl, src, dh.bitcast(fp32), ALU.subtract),
                               [T["yh", s, b], g_(("cc", pt, 2))], "v_yl")

        def step_c(t, c, k):
            ys = t % YR
            c0, w_ = CH[c]
            ms = []
            for n_, (w, m) in enumerate(((yh, Wh), (yh, Wl), (yl, Wh))):
                ms.append(lambda e, w=w, m=m, n_=n_: e.matmul(O[c][:, 0:w_], w[:, ys, k, :], m[:, k, c0:c0 + w_],
                                                             start=k == 0 and n_ == 0, stop=k == 7 and n_ == 2))
            T["cc", t, c] = do("pe", seq(*ms), [g_(("yl", t // 2, 2 * (t % 2) + 1)), g_(("f", t - 1, c)), w_done,
                                                g_(("zst", t)) if c == 2 else None], "p_cc")

        def unit_zc(t):
            z = O[0][:, 4:36].rearrange("p (e r) -> p e r", e=E)
            a = do("dve", lambda e: e.tensor_tensor(lg[:, :], O[0][:, 0:4], ebb[:, :], ALU.add), [T["cc", t, 0]], "v_z")
            a = do("dve", lambda e: e.reduce_max(mx[:, :], lg[:, :], AX.X), [a], "v_z")
            a = do("dve", lambda e: e.scalar_tensor_tensor(out=sc[:, :], in0=lg[:, :], scalar=mx[:, 0:1], in1=wts[:, :],
                                                           op0=ALU.is_equal, op1=ALU.mult), [a, d_on], "v_z")
            a = do("dve", lambda e: e.reduce_max(m2[:, :], sc[:, :], AX.X), [a], "v_z")
            a = do("dve", lambda e: e.scalar_tensor_tensor(
                out=zm[:, :].rearrange("p (e r) -> p e r", e=E), in0=sc[:, :].unsqueeze(2).broadcast_to([128, E, R]),
                scalar=m2[:, 0:1], in1=z, op0=ALU.is_equal, op1=ALU.mult), [a], "v_z")
            zz = zs[:, :].rearrange("p (t n) -> p t n", t=3)
            a = do("dve", lambda e: e.tensor_copy(zz[:, 0::2, :].bitcast(f32r), zm[:, :].unsqueeze(1).broadcast_to([128, 2, 32])),
                   [a, g_(("zt", t - 1))], "v_z")
            T["zc", t] = do("dve", lambda e: e.tensor_tensor(zz[:, 1, :].bitcast(f32r), zm[:, :], zz[:, 0, :], ALU.subtract), [a], "v_z")

        def unit_zt(t):
            T["zt", t] = do("pe", lambda e: e.transpose(O[2][0:96, 0:128], zs[:, :], ident[:, :]), [T["zc", t], g_(("f", t - 1, 2))], "p_zt")
            T["zst", t] = do("act", lambda e: e.activation(zst[:, :], O[2][0:96, 0:128], ACT.Copy), [T["zt", t], g_(("dl", t - 1, 2))], "a_zt")

        def unit_dl(t, c):
            n0, w_ = 8 * A0[c], 8 * NA[c]
            T["dl", t, c] = do("pe", lambda e: e.matmul(O[c][:, OFF[c]:OFF[c] + w_], zst[:, :], Ls[:, n0:n0 + w_], start=False, stop=True,
                                                        skip_group_check=True), [T["zst", t], l_s], "p_dl")

        def unit_f(t, c):
            n0, na = 8 * A0[c], NA[c]
            src = O[c][:, OFF[c]:OFF[c] + 8 * na].rearrange("p (a c) -> p a c", c=8)
            dst = osb[:, n0:n0 + 8 * na].rearrange("p (a c) -> p a c", c=8)
            xs = x1[:, t % XR].rearrange("p r j -> p j r")
            do("dve", lambda e: e.tensor_tensor(dst[:, :, 0:4], src[:, :, 0:4], xs[:, A0[c]:A0[c] + na, 4:8], ALU.add),
               [T["dl", t, c], g_(("st", t - 1)), T["x1", t // 2, 2 * (t % 2) + 1]])
            T["f", t, c] = do("dve", lambda e: e.tensor_tensor(dst[:, :, 4:8], src[:, :, 4:8], xs[:, A0[c] + 1:A0[c] + 1 + na, 0:4], ALU.add),
                              (), "v_f")
            if c == 2:
                T["st", t] = do("sp", lambda e: e.dma_start(out_v[t], osb[:, :]), [T["f", t, 2]], "d_st", 16)

        hooks = {}

        def hook(n_, fn, *a):
            hooks.setdefault(n_, []).append((fn, a))

        for q in range(2):
            hook(24 * q + 7, "zc", q)
            hook(24 * q + 14, "zt", q)
            hook(24 * q + 17, "dl", q, 0)
            hook(24 * q + 23, "dl", q, 1)
            hook(24 * q + 23, "dl", q, 2)
        A_AT = PLAN["A"]
        for name, at in PLAN.items():
            for n_, a in at:
                hook(n_, name, *a)

        load_x(0)
        load_ag(0)
        for it in range(-2, NS):
            sa, sb_ = it + 2, it + 1
            for n_ in range(48):
                if it >= 0:
                    step_c(2 * it + n_ // 24, n_ % 24 // 8, n_ % 8)
                for name, a in hooks.get(n_, ()):
                    if name == "A":
                        if sa < NS:
                            kind, *arg = a
                            dict(tx=unit_tx, u=unit_u, tu=unit_tu, v=unit_v, xb=unit_xb, o=unit_o)[kind](sa, *arg)
                            if kind == "v" and sa + 1 < NS:
                                load_ag(sa + 1)
                            if kind == "xb" and arg[0] == 1 and sa + 1 < NS:
                                load_x(sa + 1)
                    elif name == "B":
                        if 0 <= sb_ < NS:
                            kind, *arg = a
                            dict(xs=unit_xs, c=unit_c, td=unit_td)[kind](sb_, *arg)
                    elif it >= 0:
                        t = 2 * it + a[0]
                        if name == "zc":
                            unit_zc(t)
                        elif name == "zt":
                            unit_zt(t)
                        else:
                            unit_dl(t, a[1])
                            unit_f(t, a[1])
        do("sp", lambda e: e.nop(), [("d_st", 16 * 2 * NS), ("d_agw", 48), ("d_tapw", 16)])

        block = ctx.enter_context(nc.Block())

        @block.sync
        def _(eng):
            play("sp", eng)

        @block.gpsimd
        def _(eng):
            play("pool", eng)

        @block.scalar
        def _(eng):
            play("act", eng)

        @block.vector
        def _(eng):
            play("dve", eng)

        @block.tensor
        def _(eng):
            play("pe", eng)


PLAN = {
    "A": [(0, ("xb", 0)), (0, ("tx", 0)), (2, ("tx", 1)), (4, ("tx", 2)), (6, ("tx", 3)),
          (10, ("u", 0)), (12, ("u", 1)), (14, ("tu",)), (18, ("v",)),
          (28, ("xb", 1)), (29, ("o", 0)), (31, ("o", 1)), (37, ("o", 2)), (39, ("o", 3))],
    "B": [(9, ("xs",)), (20, ("c", 0)), (22, ("c", 1)), (24, ("c", 2)), (26, ("c", 3)),
          (33, ("td", 0)), (35, ("td", 1)), (41, ("td", 2)), (43, ("td", 3))],
}

_INS = ['x', 'cond_128', 'fside_S_0', 'L0_cond_W0', 'L0_cond_b0', 'L0_cond_W1', 'L0_cond_b1', 'L0_cond_W2', 'L0_cond_b2',
        'L0_cond_weight', 'L0_cond_bias_k', 'L0_ffn_A', 'L0_ffn_B', 'L0_ffn_bias', 'L1_cond_weight', 'L1_cond_c_weight',
        'L1_ffn_W_up', 'L1_ffn_gate_w', 'L1_ffn_expert_bias', 'L1_ffn_lora_A', 'L1_ffn_lora_B']


def kernel(**inputs):
    import numpy as _np
    import concourse.bacc as _bacc
    from concourse import mybir as _mybir
    from concourse.bass_utils import run_bass_kernel_spmd as _run

    nc = _bacc.Bacc("TRN2", target_bir_lowering=False, num_devices=1)
    arrays, args = {}, []
    for name in _INS:
        a = _np.ascontiguousarray(inputs[name])
        arrays[f"in_{name}_dram"] = a
        args.append(nc.dram_tensor(f"in_{name}_dram", a.shape, _mybir.dt.from_np(a.dtype), kind="ExternalInput").ap())
    o = nc.dram_tensor("out_0_dram", (NB, C, L), _mybir.dt.float32, kind="ExternalOutput").ap()
    adaln_ffn(nc, *args, o)
    r = _run(nc, [arrays], core_ids=[0])
    return r.results[0]["out_0_dram"]
```

```python
import concourse.bass as bass
from concourse import mybir
from contextlib import ExitStack

NB = 128
C = 64
L = 1024
RK = 128
E = 4
R = 8
NG = 4
NS = 32
WC = 36 + L
CH = [(0, 380), (380, 344), (724, 336)]
OFF = [36, 0, 0]
NA = [43, 43, 42]
A0 = [0, 43, 86]
XR = 5
YR = 3


def adaln_ffn(nc, x, cond, fside, W0, b0, W1, b1, W2, b2, wk, bias_k, A, B, fbias,
              cw, ccw, Wup, gate, ebias, loA, loB, out):
    fp32 = mybir.dt.float32
    f32r = mybir.dt.float32r
    ALU = mybir.AluOpType
    ACT = mybir.ActivationFunctionType
    AX = mybir.AxisListType

    x_v = x.rearrange("b c l -> (b c) l").rearrange("(s q p) l -> s p q l", q=2, p=128)
    z_v = x.rearrange("b c l -> (b c) l").rearrange("(s t i) l -> s i t l", t=8, i=32)
    out_v = out.rearrange("b c l -> (b c) l").rearrange("(t p) l -> t p l", p=128)
    aggD = nc.dram_tensor("agg_scratch", (NB, C, C), fp32, kind="Internal").ap()
    agbD = nc.dram_tensor("agb_scratch", (NB, C), fp32, kind="Internal").ap()
    tapD = nc.dram_tensor("tap_scratch", (C, 16, 24), fp32, kind="Internal").ap()

    ctx = ExitStack()
    with ctx:
        place = {"": (nc.sbuf_base + 31) // 32 * 32}

        def sb(name, shape, dt=fp32):
            size = 4
            for n in shape[1:]:
                size *= n
            place[name] = place[""]
            place[""] += (size + 31) // 32 * 32
            assert place[""] <= nc.sbuf_usable_end
            return nc.alloc_sbuf_tensor_at(name, shape, dt, offset=place[name])

        def over(name, base, shape, start=0):
            return nc.alloc_sbuf_tensor_at(name, shape, fp32, offset=place[base] + 4 * start)

        Wh = sb("Wh", [128, 8, WC], f32r)
        Wl = sb("Wl", [128, 8, WC], f32r)
        Ah = sb("Ah", [128, 8, 128], f32r)
        Al = sb("Al", [128, 8, 128], f32r)
        Bh = sb("Bh", [128, 8, RK], f32r)
        Bl = sb("Bl", [128, 8, RK], f32r)
        Th = sb("Th", [128, NG, 2, 8, 16], f32r)
        Tl = sb("Tl", [128, NG, 2, 8, 16], f32r)
        Ls = sb("Ls", [96, L], f32r)
        biasb = sb("biasb", [128, L])
        ident = sb("ident", [128, 128])
        cb = sb("cb", [128, NB, NG])
        csB = sb("csB", [128, 1])
        ebb = sb("ebb", [128, E])
        wts = sb("wts", [128, E])
        xin = sb("xin", [128, 2, L])
        xTh = sb("xTh", [128, 8, 256], f32r)
        xTl = sb("xTl", [128, 8, 256], f32r)
        xTr = over("xTr", "xTl", [128, 8, 256])
        zin = sb("zin", [128, 8, 256])
        D = sb("D", [128, 2, 512])
        u = sb("u", [128, 256])
        agg = sb("agg", [128, 2, 128])
        agb = sb("agb", [128, 256])
        vh = sb("vh", [128, 256], f32r)
        vl = sb("vl", [128, 256], f32r)
        v = over("v", "vl", [128, 256])
        x1 = sb("x1", [128, XR, 8, 129])
        Xlo = sb("Xlo", [128, 4, NG, 129], f32r)
        Xhi = sb("Xhi", [128, 4, NG, 129], f32r)
        yh = sb("yh", [128, YR, 8, 128], f32r)
        yl = sb("yl", [128, YR, 8, 128], f32r)
        yr = over("yr", "yl", [128, YR, 8, 128])
        osb = sb("osb", [128, L])
        lg = sb("lg", [128, E])
        mx = sb("mx", [128, 1])
        sc = sb("sc", [128, E])
        m2 = sb("m2", [128, 1])
        zm = sb("zm", [128, E * R])
        zs = sb("zs", [128, 96])
        zst = sb("zst", [96, 128], f32r)

        O = [ctx.enter_context(nc.psum_tensor(f"O{i}", [128, 512], fp32)) for i in range(3)]
        F = [ctx.enter_context(nc.psum_tensor(f"F{i}", [128, 512], fp32)) for i in range(5)]
        P = O + F

        queues = {e: [] for e in ("pe", "act", "dve", "pool", "sp")}
        sems, counts = {}, {}

        def do(engine, emit, after=(), sem=None, by=1):
            queues[engine].append((emit, [a for a in after if a], sem, by))
            if sem is None:
                return None
            if sem not in sems:
                sems[sem] = ctx.enter_context(nc.semaphore(sem))
                counts[sem] = 0
            counts[sem] += by
            return sem, counts[sem]

        def play(engine, eng):
            known = {}
            for emit, after, sem, by in queues[engine]:
                for name, value in after:
                    if known.get(name, 0) < value:
                        eng.wait_ge(sems[name], value)
                        known[name] = value
                ins = emit(eng)
                if sem is not None:
                    ins.then_inc(sems[sem], by)

        def load(dst, src, after=(), sem="d_set"):
            return do("sp", lambda e: e.dma_start(dst, src), after, sem, 16)

        def seq(*emits):
            def go(e):
                for f in emits:
                    last = f(e)
                return last
            return go

        T = {}
        evac = {}

        def g_(key):
            if key[1] < 0 or (key[0] == "u" and key[1] >= NS):
                return None
            return T[key]

        small = over("small", "Wl", [128, 1472], 4096)
        cnd = small[:, 0:128]
        W0s = small[:, 128:256]
        W1s = small[:, 256:384]
        W2s = small[:, 384:392]
        b2s = small[:, 392:400]
        b0s = small[:, 400:401]
        b1s = small[:, 401:402]
        fsc = small[:, 404:408]
        cwn = small[0:64, 512:640]
        bks = small[0:8, 640:704]
        condT = small[:, 768:896]
        h1 = small[:, 896:1024]
        h2 = small[:, 1024:1152]
        att = small[:, 1152:1160]
        atn = small[:, 1160:1168]
        nmx = small[:, 1168:1169]
        ssum = small[:, 1169:1170]
        rs = small[:, 1170:1171]
        ones = small[:, 1171:1172]
        attT = small[0:8, 1184:1312]
        ccT = small[:, 1312:1376]
        agbs = small[:, 1408:1472]
        aggS = over("aggS", "Wl", [128, 2, C, 32])
        wks = over("wks", "Wh", [8, 4096])
        Uw = over("Uw", "Wh", [128, C, 16], 4096)
        taps = over("taps", "Wh", [64, 16, 24], 5120)
        tapn = over("tapn", "Wh", [64, 16, 9], 5504)
        cwX = over("cwX", "Wh", [128, NG, 8, 16], 5648)
        Braw = over("Braw", "Xlo", [128, 8, RK])
        Araw = over("Araw", "Xlo", [128, 8, RK], 1024)
        LBr = over("LBr", "Xhi", [128, 8, E, R])
        LB3 = over("LB3", "Xhi", [128, 8, 3, E * R], 256)
        Graw = over("Graw", "Xhi", [36, L], 1024)
        ya, yb = over("ya", "yh", [128, YR, L]), over("yb", "yl", [128, YR, L])
        x1s = over("x1s", "x1", [128, L], 4 * 8 * 129)
        raw = [x1s[:, :], osb[:, :], ya[:, 1, :], yb[:, 1, :]]
        srt = [ya[:, 2, :], yb[:, 2, :], ya[:, 0, :], yb[:, 0, :]]

        do("pool", lambda e: e.memset(ident[:, :], 0.0), sem="g_id")
        g_id = do("pool", lambda e: e.affine_select(out=ident[:, :], in_=ident[:, :], compare_op=ALU.not_equal,
                                                    fill=1.0, base=0, pattern=[[-1, 128]], channel_multiplier=1),
                  [("g_id", 1)], "g_id")
        g_tap = do("pool", lambda e: e.memset(taps[:, :, :], 0.0), sem="g_id")
        for i in range(E):
            do("pool", lambda e, i=i: e.memset(wts[:, i:i + 1], float(E - i)))
        do("pool", lambda e: e.memset(agg[:, :, :], 0.0))
        do("pool", lambda e: e.memset(x1[:, 0:4, 0:4, 0:1], 0.0))
        do("pool", lambda e: e.memset(x1[:, 0:4, 4:8, 128:129], 0.0))
        g_con = do("pool", lambda e: e.memset(ones, 1.0), sem="g_id")

        l_c = load(cnd, cond, sem="d_cnd")
        load(W0s, W0, sem="d_mlp")
        load(b0s, b0.rearrange("(p a) -> p a", a=1), sem="d_mlp")
        load(W1s, W1, sem="d_mlp")
        load(b1s, b1.rearrange("(p a) -> p a", a=1), sem="d_mlp")
        load(W2s, W2, sem="d_mlp")
        l_m = load(b2s, b2.rearrange("(a k) -> a k", a=1).broadcast_to([128, 8]), sem="d_mlp")
        l_t = load(tapn[:, :, :], cw, sem="d_tap")

        def load_x(s):
            T["x", s] = do("sp", lambda e: e.dma_start(xin[:, :, :], x_v[s]), [g_(("xb", s - 1, 1))], "d_x", 16)

        def load_z(s):
            for a in range(4):
                T["z", s] = do("sp", lambda e, a=a: e.dma_start(zin[32 * a:32 * a + 32, :, :], z_v[s, :, :, 256 * a:256 * a + 256]),
                               [g_(("tz", s - 1, 1))], "d_z", 16)

        load_z(0)
        for a in range(4):
            l_b = load(Braw[32 * a:32 * a + 32, :, :], B[256 * a:256 * a + 256, :].rearrange("(c i) k -> i c k", i=32), sem="d_b")
        load(wks[:, :], wk.rearrange("k o i a -> k (o i a)"), sem="d_wk")
        l_k = load(bks, bias_k, sem="d_wk")

        for k in range(9):
            v_tap = do("dve", lambda e, k=k: e.tensor_copy(taps[:, :, 15 - k:16 - k], tapn[:, :, k:k + 1]), [l_t, g_tap], "v_tap")
        d_tap = do("sp", lambda e: e.dma_start(tapD, taps[:, :, :]), [v_tap], "d_tapw", 16)

        load_x(0)
        l_a = load(Araw[:, :, :], A.rearrange("(j c) k -> j c k", c=8), sem="d_a")
        l_bi = load(biasb[:, :], fbias.rearrange("(a n) -> a n", a=1).broadcast_to([128, L]), sem="d_bi")
        for r in range(8):
            l_u = load(Uw[r::8, :, :], tapD[:, :, 7 - r:23 - r].rearrange("o i m -> i o m"), [d_tap], "d_tapr")
        load(cwn, ccw, sem="d_cc")
        for r in range(8):
            l_cc = do("sp", lambda e, r=r: e.dma_start(fsc[16 * r:16 * r + 16, :], fside.rearrange("(g o) -> o g", o=16),
                                                       allow_slow_non_contiguous=True), (), "d_cc", 16)

        pc = do("pe", lambda e: e.transpose(F[4][:, 0:128], cnd, ident[:, :]), [l_c, g_id], "p_mlp")
        ac = do("act", lambda e: e.activation(condT, F[4][:, 0:128], ACT.Copy), [pc], "a_mlp")
        p1 = do("pe", lambda e: e.matmul(F[4][:, 128:256], W0s, condT, start=True, stop=True), [ac, l_m], "p_mlp")
        a1 = do("act", lambda e: e.activation(h1, F[4][:, 128:256], ACT.Gelu, bias=b0s), [p1], "a_mlp")
        p2 = do("pe", lambda e: e.matmul(F[4][:, 256:384], W1s, h1, start=True, stop=True), [a1], "p_mlp")
        a2 = do("act", lambda e: e.activation(h2, F[4][:, 256:384], ACT.Gelu, bias=b1s), [p2], "a_mlp")
        p3 = do("pe", lambda e: e.matmul(F[4][:, 384:392], h2, W2s, start=True, stop=True), [a2], "p_mlp")
        w1 = do("dve", lambda e: e.tensor_tensor(att, F[4][:, 384:392], b2s, ALU.add), [p3, l_m], "v_mlp")
        w2 = do("dve", lambda e: e.tensor_reduce(nmx, att, AX.X, ALU.max, negate=True), [w1], "v_mlp")
        a3 = do("act", lambda e: e.activation(atn, att, ACT.Exp, bias=nmx, accum_out=ssum), [w2], "a_mlp")
        w3 = do("dve", lambda e: e.reciprocal(rs, ssum), [a3], "v_mlp")
        w4 = do("dve", lambda e: e.tensor_scalar(att, atn, rs, None, ALU.mult), [w3, a3], "v_mlp")
        p4 = do("pe", lambda e: e.transpose(F[3][0:8, 0:128], att, ident[:, :]), [w4], "p_mlp")
        w5 = do("dve", lambda e: e.tensor_copy(attT, F[3][0:8, 0:128]), [p4], "v_mlp")
        G6 = [O[0], O[1], O[2], F[0], F[1], F[2]]
        v_ag = []
        for c in range(8):
            bank = G6[c % 6]
            pg = do("pe", lambda e, c=c, bank=bank: e.matmul(bank[:, :], attT, wks[:, 512 * c:512 * c + 512], start=True, stop=True),
                    [w5, l_k, v_ag[c - 6] if c >= 6 else None], "p_ag")
            dst = aggS[:, c // 4, :, 8 * (c % 4):8 * (c % 4) + 8].rearrange("p i o -> p o i")
            src = bank[:, :].rearrange("p (o i) -> p o i", o=8)
            if c % 2:
                v_ag.append(do("act", lambda e, dst=dst, src=src: e.activation(dst, src, ACT.Copy), [pg], "a_ag"))
            else:
                v_ag.append(do("dve", lambda e, dst=dst, src=src: e.tensor_copy(dst, src), [pg], "v_ag"))
        pb = do("pe", lambda e: e.matmul(F[4][:, 0:64], attT, bks, start=True, stop=True), [w5, l_k], "p_ag")
        v_b = do("dve", lambda e: e.tensor_copy(agbs, F[4][:, 0:64]), [pb], "v_ag")
        for h in range(2):
            do("sp", lambda e, h=h: e.dma_start(aggD[:, :, 32 * h:32 * h + 32], aggS[:, h]), [v_ag[4 * h + 2], v_ag[4 * h + 3]], "d_agw", 16)
        d_agw = do("sp", lambda e: e.dma_start(agbD, agbs), [v_b], "d_agw", 16)

        b_h = do("act", lambda e: e.activation(Bh[:, :, :], Braw[:, :, :], ACT.Copy), [l_b], "a_b")
        b_l = do("dve", lambda e: e.tensor_tensor(Bl[:, :, :], Braw[:, :, :], Bh[:, :, :].bitcast(fp32), ALU.subtract), [b_h], "v_b")
        pcs = do("pe", seq(*[lambda e, c=c: e.matmul(F[3][:, 0:1], Braw[:, c, :], ones, start=c == 0, stop=c == 7)
                             for c in range(8)]), [l_b, g_con, w5], "p_b")
        csb = do("dve", lambda e: e.tensor_copy(csB[:, :], F[3][:, 0:1]), [pcs], "v_b")

        def setup_a():
            for h in range(2):
                pa = do("pe", seq(*[lambda e, h=h, c=c: e.transpose(F[h][:, 128 * c:128 * c + 128], Araw[:, 4 * h + c, :], ident[:, :])
                                    for c in range(4)]), [l_a, v_ag[3 + h]], "p_a")
                dh, dl = (t_[:, 4 * h:4 * h + 4, :].rearrange("p a b -> p (a b)") for t_ in (Ah, Al))
                ah = do("act", lambda e, h=h, dh=dh: e.activation(dh, F[h][:, :], ACT.Copy), [pa], "a_a")
                evac[h] = T["al"] = do("dve", lambda e, h=h, dh=dh, dl=dl: e.tensor_tensor(dl, F[h][:, :], dh.bitcast(fp32), ALU.subtract),
                                       [ah], "v_a")
            T["pa"] = pa

        def setup_taps():
            for blk in range(2):
                src = Uw[:, :, 8 - 8 * blk:16 - 8 * blk].rearrange("p (g o) r -> p g r o", g=NG)
                t_h = [do("dve", lambda e, g=g, blk=blk, src=src: e.tensor_copy(Th[:, g, blk], src[:, g]), [l_u], "v_t")
                       for g in range(NG)]
                for g in range(NG):
                    T["t"] = do("dve", lambda e, g=g, blk=blk, src=src: e.tensor_tensor(
                        Tl[:, g, blk], src[:, g], Th[:, g, blk].bitcast(fp32), ALU.subtract), [t_h[g]], "v_t")

        def setup_cb():
            pcc = do("pe", lambda e: e.transpose(F[2][:, 0:64], cwn, ident[0:64, 0:64]), [l_cc, v_ag[5]], "p_cb")
            acc = do("dve", lambda e: e.tensor_copy(ccT, F[2][:, 0:64]), [pcc], "v_cb")
            for g in range(NG):
                vx = do("dve", lambda e, g=g: e.tensor_copy(cwX[:, g], ccT[:, 16 * g:16 * g + 16].unsqueeze(1).broadcast_to([128, 8, 16])),
                        [acc], "v_cb")
            for g in range(NG):
                T["pcb"] = do("pe", lambda e, g=g: e.matmul(F[2][:, 128 * g:128 * g + 128], cwX[:, g].rearrange("p r o -> p (r o)"), condT,
                                                            start=True, stop=True), [vx], "p_cb")
            for g in range(NG):
                evac[2] = T["cb"] = do("dve", lambda e, g=g: e.tensor_scalar(cb[:, :, g], F[2][:, 128 * g:128 * g + 128],
                                                                             fsc[:, g:g + 1], None, ALU.add), [T["pcb"], l_cc], "v_cb")

        def sorted_copy(dst, src, after, sem):
            for r in range(2):
                d_ = dst.rearrange("p (b r q i) -> p b r q i", b=4, r=2, q=4)[:, :, r]
                s_ = src.rearrange("p (b i q r) -> p b r q i", b=4, i=32, q=4)[:, :, r]
                t_ = do("act", lambda e, d_=d_, s_=s_: e.activation(d_, s_, ACT.Copy), after, sem)
            return t_

        def load_lora():
            do("sp", lambda e: e.dma_start(ebb[:, :], ebias.rearrange("(a n) -> a n", a=1).broadcast_to([128, E])), (), "d_lo", 16)
            do("sp", lambda e: e.dma_start(Graw[0:4, :], gate), (), "d_lo", 16)
            do("sp", lambda e: e.dma_start(Graw[4:36, :], loA.rearrange("e r h -> (e r) h")), (), "d_lo", 16)
            for e_ in range(E):
                T["lo"] = load(LBr[:, :, e_, :], loB[e_].rearrange("(m p) r -> p m r", p=128), sem="d_lo")

        def setup_lora():
            LB2 = LBr[:, :, :, :].rearrange("p m e r -> p m (e r)")
            for t in range(2):
                l_h = do("dve", lambda e, t=t: e.tensor_copy(LB3[:, :, t, :].bitcast(f32r), LB2), [T["lo"]], "v_lo")
            l_l = do("dve", lambda e: e.tensor_tensor(LB3[:, :, 2, :].bitcast(f32r), LB2, LB3[:, :, 0, :], ALU.subtract), [l_h], "v_lo")
            for h in range(2):
                pl = do("pe", seq(*[lambda e, h=h, m=m: e.transpose(O[h][0:96, 128 * m:128 * m + 128],
                                                                   LB3[:, 4 * h + m].rearrange("p t n -> p (t n)"), ident[:, :])
                                    for m in range(4)]), [l_l, v_ag[7], v_ag[6]], "p_lo")
                T["ls"] = do("act", lambda e, h=h: e.activation(Ls[:, 512 * h:512 * h + 512], O[h][0:96, :], ACT.Copy), [pl], "a_lo")
            gs = sorted_copy(ya[0:36, 2, :], Graw[:, :], [T["lo"]], "a_lo")
            pg = do("pe", seq(*[lambda e, c=c: e.transpose(O[2][:, 36 * c:36 * c + 36], ya[0:36, 2, 128 * c:128 * c + 128], ident[0:36, 0:36])
                                for c in range(8)]), [gs, v_ag[2]], "p_lo")
            src = O[2][:, 0:288].rearrange("p (c n) -> p c n", c=8)
            done = [pg, d_agw, T["t"], T["pcb"], T["cb"], csb, v_tap, d_tap]
            gh = do("act", lambda e: e.activation(Wh[:, :, 0:36], src, ACT.Copy), done, "a_lo")
            T["g"] = do("dve", lambda e: e.tensor_tensor(Wl[:, :, 0:36], src, Wh[:, :, 0:36].bitcast(fp32), ALU.subtract), [gh], "v_lo")
            T["pg"] = pg
            T["small"] = done

        def load_w(m):
            T["wl", m] = load(raw[m % 4], Wup[128 * m:128 * m + 128, :], [T.get(("ws", m - 4))], f"d_w{m % 4}")

        def sort_w(m):
            T["ws", m] = sorted_copy(srt[m % 4], raw[m % 4], [T["wl", m], T.get(("pw", m - 4)), T["pg"]], "a_ws")

        def setup_w(m):
            for h in range(2):
                half_w(m, h, O[(2 * m + h) % 3])

        def half_w(m, h, bank):
            n = 2 * m + h
            T["pw", m] = do("pe", seq(*[lambda e, c=c: e.transpose(
                bank[:, 128 * c:128 * c + 128], srt[m % 4][:, 512 * h + 128 * c:512 * h + 128 * c + 128], ident[:, :])
                for c in range(4)]), [T["ws", m], T.get(("w", n - 3)), T["g"], T["ls"]], "p_w")
            dh, dl = (t_[:, 4 * h:4 * h + 4, 36 + 128 * m:164 + 128 * m] for t_ in (Wh, Wl))
            src = bank[:, :].rearrange("p (c n) -> p c n", c=4)
            aw = do("act", lambda e: e.activation(dh, src, ACT.Copy), [T["pw", m]] + T["small"], "a_w")
            T["w", n] = do("dve", lambda e: e.tensor_tensor(dl, src, dh.bitcast(fp32), ALU.subtract), [aw], "v_w")

        def setup_pad():
            do("pool", lambda e: e.memset(x1[:, 4, 0:4, 0:1], 0.0), [T["ws", 4]])
            T["pad"] = do("pool", lambda e: e.memset(x1[:, 4, 4:8, 128:129], 0.0), [T["ws", 4]], "g_pad")

        def load_ag(s):
            prev = [g_(("v", s - 1)), g_(("vv", s - 1))] + ([d_agw, g_con] if s == 0 else [])
            for b in range(2):
                src = aggD[4 * s + b:4 * s + b + 3:2].rearrange("q c o -> c q o")
                do("sp", lambda e, b=b, src=src: e.dma_start(agg[64 * b:64 * b + 64, :, 64 * b:64 * b + 64], src), prev, "d_ag", 16)
            src = agbD[4 * s:4 * s + 4, :].rearrange("(a b) o -> a (b o)", a=1).broadcast_to([128, 256])
            T["ag", s] = do("sp", lambda e: e.dma_start(agb[:, :], src), prev, "d_ag", 16)

        def unit_tz(s, q):
            src = zin[:, 4 * q:4 * q + 4, :].rearrange("p t (k i) -> p t k i", i=32)
            dst = xTr[:, :, 128 * q:128 * q + 128].rearrange("p k (t i) -> p t k i", i=32)
            T["tz", s, q] = do("dve", lambda e: e.transpose(dst, src), [T["z", s], g_(("u", s - 1)), g_(("txl", s - 1, q))], "v_tz")
            dh, dl, dr = (t_[:, :, 128 * q:128 * q + 128] for t_ in (xTh, xTl, xTr))
            T["txh", s, q] = do("act", lambda e: e.activation(dh, dr, ACT.Copy), [T["tz", s, q], g_(("u", s - 1))], "a_txh")
            T["txl", s, q] = do("pool", lambda e: e.tensor_tensor(dl, dr, dh.bitcast(fp32), ALU.subtract), [T["txh", s, q]], "g_txl")

        def unit_u(s, half):
            ms = []
            for c in range(4 * half, 4 * half + 4):
                for n_, (w, m) in enumerate(((Bh, xTh), (Bh, xTl), (Bl, xTh))):
                    ms.append(lambda e, c=c, w=w, m=m, n_=n_: e.matmul(F[4][:, 0:256], w[:, c, :], m[:, c, :],
                                                                      start=c == 0 and n_ == 0, stop=c == 7 and n_ == 2))
            T["u", s] = do("pe", seq(*ms), [T["txl", s, 0], T["txl", s, 1], g_(("vv", s - 1)), b_h, b_l, v_b], "p_u")
            if half:
                T["ut", s] = do("act", lambda e: e.activation(u[:, :], F[4][:, 0:256], ACT.Copy), [T["u", s], g_(("v", s - 1))], "a_u")

        def unit_tu(s):
            T["tu", s] = do("pe", seq(*[lambda e, q=q: e.transpose(F[4][:, 128 * q:128 * q + 128], u[:, 128 * q:128 * q + 128], ident[:, :])
                                        for q in range(2)]), [T["ut", s]], "p_tu")
            T["tuu", s] = do("act", lambda e: e.activation(u[:, :], F[4][:, 0:256], ACT.Copy), [T["tu", s]], "a_tu")

        def unit_v(s):
            T["v", s] = do("pe", seq(*[lambda e, q=q: e.matmul(F[4][:, 128 * q:128 * q + 128], u[:, 128 * q:128 * q + 128], agg[:, q, :],
                                                               start=True, stop=True) for q in range(2)]),
                           [T["tuu", s], T["ag", s]], "p_v")
            T["vv", s] = do("dve", lambda e: e.scalar_tensor_tensor(out=v[:, :], in0=agb[:, :], scalar=csB[:, 0:1], in1=F[4][:, 0:256],
                                                                    op0=ALU.mult, op1=ALU.add),
                            [T["v", s], T["ag", s], g_(("vh", s - 1)), csb, g_(("vl", s - 1)), g_(("o", s - 1, 3))], "v_v")
            T["vh", s] = do("act", lambda e: e.activation(vh[:, :], v[:, :], ACT.Copy), [T["vv", s], g_(("o", s - 1, 3))], "a_vh")
            T["vl", s] = do("dve", lambda e: e.tensor_tensor(vl[:, :], v[:, :], vh[:, :].bitcast(fp32), ALU.subtract),
                            [T["vh", s], g_(("o", s - 1, 3))], "v_vl")

        def slot(s, q):
            return (2 * s + q) % XR

        def unit_xb(s, q):
            t = 2 * s + q
            xs = xin[:, q, :].rearrange("p (a c) -> p c a", c=8)
            bs = biasb[:, :].rearrange("p (a c) -> p c a", c=8)
            o = x1[:, slot(s, q)]
            for h in range(2):
                dst = o[:, 4:8, 0:128] if h == 0 else o[:, 0:4, 1:129]
                T["xb", s, q] = do("pool", lambda e, h=h, dst=dst: e.tensor_tensor(dst, xs[:, 4 * h:4 * h + 4, :], bs[:, 4 * h:4 * h + 4, :], ALU.add),
                                   [T["x", s], g_(("f", t - XR, 2)), g_(("rx", (t - XR) // 2, (t - XR) % 2)), l_bi, T["pad"] if t == 4 else None], "g_xb")

        def unit_o(s, i):
            q, h = i // 2, i % 2
            ms = []
            for n_, (w, m) in enumerate(((vh, Ah), (vh, Al), (vl, Ah))):
                ms.append(lambda e, w=w, m=m, n_=n_: e.matmul(F[i][:, :], w[:, 128 * q:128 * q + 128],
                                                             m[:, 4 * h:4 * h + 4, :].rearrange("p c a -> p (c a)"),
                                                             start=n_ == 0, stop=n_ == 2))
            T["o", s, i] = do("pe", seq(*ms), [T["vl", s], evac.get(i), T["al"], csb], "p_o")
            o = x1[:, slot(s, q)]
            dst = o[:, 4:8, 0:128] if h == 0 else o[:, 0:4, 1:129]
            evac[i] = T["x1", s, i] = do("dve", lambda e: e.tensor_tensor(dst, F[i][:, :].rearrange("p (c a) -> p c a", c=4), dst, ALU.add),
                               [T["o", s, i], T["xb", s, q]], "v_x1")

        def unit_rx(s, q):
            for b in range(2):
                for g in range(NG):
                    p0 = 64 * b + 16 * g
                    T["rx", s, q] = do("sp", lambda e, b=b, g=g, p0=p0: e.dma_start(
                        Xlo[:, 2 * q + b, g, :].bitcast(fp32), x1[p0:p0 + 16, slot(s, q), :, :]),
                        [T["x1", s, 2 * q], T["x1", s, 2 * q + 1], g_(("c", s - 1, 3)), b_l, pcs, T["pa"]], "d_rx", 16)

        def unit_xs(s):
            T["xs1", s] = do("act", lambda e: e.activation(Xhi[:, :, :, :], Xlo[:, :, :, :].bitcast(fp32), ACT.Copy),
                             [T["rx", s, 1], g_(("c", s - 1, 3)), T["pg"]], "a_xs")
            T["xs", s] = do("dve", lambda e: e.tensor_tensor(Xlo[:, :, :, :], Xlo[:, :, :, :].bitcast(fp32),
                                                            Xhi[:, :, :, :].bitcast(fp32), ALU.subtract), [T["xs1", s]], "v_xs")

        def unit_c(s, g):
            ms = []
            for blk in range(2):
                for n_, (w, m) in enumerate(((Th, Xhi), (Tl, Xhi), (Th, Xlo))):
                    ms.append(lambda e, w=w, m=m, blk=blk, n_=n_: e.matmul(
                        F[g][:, :], w[:, g, blk].rearrange("p r o -> p (r o)"), m[:, :, g, blk:blk + 128],
                        start=blk == 0 and n_ == 0, stop=blk == 1 and n_ == 2))
            T["c", s, g] = do("pe", seq(*ms), [T["xs", s], evac.get(g), T["t"]], "p_c")
            evac[g] = T["dd", s, g] = do("dve", lambda e: e.tensor_tensor(
                D[:, g % 2, :].rearrange("p (b j) -> p b j", b=4), F[g][:, :].rearrange("p (b j) -> p b j", b=4),
                cb[:, 4 * s:4 * s + 4, g].unsqueeze(2).broadcast_to([128, 4, 128]), ALU.add),
                [T["c", s, g], T["ty", s, g - 2, 1] if g > 1 else g_(("ty", s - 1, g + 2, 1)), T["cb"]], "v_d")

        def unit_ty(s, g):
            for q in range(2):
                src = D[:, g % 2, 256 * q:256 * q + 256].rearrange("p (b i) -> p b i", i=32)
                dst = yr[:, (2 * s + q) % YR].rearrange("p (k r) (b n) -> p b k r n", r=2, b=2)[:, :, :, :, 16 * g:16 * g + 16]
                pt = 2 * s + q - YR
                T["ty", s, g, q] = do("dve", lambda e, dst=dst, src=src: e.transpose(dst, src),
                                      [T["dd", s, g], g_(("cc", pt, 2)), T["pw", 7]], "v_ty")

        def unit_ys(s, q):
            ys = (2 * s + q) % YR
            T["yh", s, q] = do("act", lambda e: e.activation(yh[:, ys], yr[:, ys], ACT.Copy),
                               [T["ty", s, 3, q], g_(("cc", 2 * s + q - YR, 2)), T["pw", 7]], "a_yh")
            T["yl", s, q] = do("dve", lambda e: e.tensor_tensor(yl[:, ys], yr[:, ys], yh[:, ys].bitcast(fp32), ALU.subtract),
                               [T["yh", s, q]], "v_yl")

        def step_c(t, c, k):
            ys = t % YR
            c0, w_ = CH[c]
            ms = []
            for n_, (w, m) in enumerate(((yh, Wh), (yh, Wl), (yl, Wh))):
                ms.append(lambda e, w=w, m=m, n_=n_: e.matmul(O[c][:, 0:w_], w[:, ys, k, :], m[:, k, c0:c0 + w_],
                                                             start=k == 0 and n_ == 0, stop=k == 7 and n_ == 2))
            T["cc", t, c] = do("pe", seq(*ms), [T["yl", t // 2, t % 2], g_(("f", t - 1, c)), T["w", 15],
                                                g_(("zst", t)) if c == 2 else None], "p_cc")

        def unit_zc(t):
            z = O[0][:, 4:36].rearrange("p (e r) -> p e r", e=E)
            a = do("dve", lambda e: e.tensor_tensor(lg[:, :], O[0][:, 0:4], ebb[:, :], ALU.add), [T["cc", t, 0], T["lo"]], "v_z")
            a = do("dve", lambda e: e.reduce_max(mx[:, :], lg[:, :], AX.X), [a], "v_z")
            a = do("dve", lambda e: e.scalar_tensor_tensor(out=sc[:, :], in0=lg[:, :], scalar=mx[:, 0:1], in1=wts[:, :],
                                                           op0=ALU.is_equal, op1=ALU.mult), [a, g_con], "v_z")
            a = do("dve", lambda e: e.reduce_max(m2[:, :], sc[:, :], AX.X), [a], "v_z")
            a = do("dve", lambda e: e.scalar_tensor_tensor(
                out=zm[:, :].rearrange("p (e r) -> p e r", e=E), in0=sc[:, :].unsqueeze(2).broadcast_to([128, E, R]),
                scalar=m2[:, 0:1], in1=z, op0=ALU.is_equal, op1=ALU.mult), [a], "v_z")
            zz = zs[:, :].rearrange("p (t n) -> p t n", t=3)
            a = do("dve", lambda e: e.tensor_copy(zz[:, 0::2, :].bitcast(f32r), zm[:, :].unsqueeze(1).broadcast_to([128, 2, 32])),
                   [a, g_(("zt", t - 1))], "v_z")
            T["zc", t] = do("dve", lambda e: e.tensor_tensor(zz[:, 1, :].bitcast(f32r), zm[:, :], zz[:, 0, :], ALU.subtract), [a], "v_z")

        def unit_zt(t):
            T["zt", t] = do("pe", lambda e: e.transpose(O[2][0:96, 0:128], zs[:, :], ident[:, :]), [T["zc", t], g_(("f", t - 1, 2))], "p_zt")
            T["zst", t] = do("act", lambda e: e.activation(zst[:, :], O[2][0:96, 0:128], ACT.Copy), [T["zt", t], g_(("dl", t - 1, 2))], "a_zt")

        def unit_dl(t, c):
            n0, w_ = 8 * A0[c], 8 * NA[c]
            T["dl", t, c] = do("pe", lambda e: e.matmul(O[c][:, OFF[c]:OFF[c] + w_], zst[:, :], Ls[:, n0:n0 + w_], start=False, stop=True,
                                                        skip_group_check=True), [T["zst", t], T["ls"]], "p_dl")

        def unit_f(t, c):
            n0, na = 8 * A0[c], NA[c]
            src = O[c][:, OFF[c]:OFF[c] + 8 * na].rearrange("p (a c) -> p a c", c=8)
            dst = osb[:, n0:n0 + 8 * na].rearrange("p (a c) -> p a c", c=8)
            xs = x1[:, t % XR].rearrange("p r j -> p j r")
            do("dve", lambda e: e.tensor_tensor(dst[:, :, 0:4], src[:, :, 0:4], xs[:, A0[c]:A0[c] + na, 4:8], ALU.add),
               [T["dl", t, c], g_(("st", t - 1)), T["x1", t // 2, 2 * (t % 2) + 1]])
            T["f", t, c] = do("dve", lambda e: e.tensor_tensor(dst[:, :, 4:8], src[:, :, 4:8], xs[:, A0[c] + 1:A0[c] + 1 + na, 0:4], ALU.add),
                              (), "v_f")
            if c == 2:
                T["st", t] = do("sp", lambda e: e.dma_start(out_v[t], osb[:, :]), [T["f", t, 2]], "d_st", 16)

        hooks = {}

        def hook(n_, fn, *a):
            hooks.setdefault(n_, []).append((fn, a))

        for q in range(2):
            hook(24 * q + 7, "zc", q)
            hook(24 * q + 14, "zt", q)
            hook(24 * q + 17, "dl", q, 0)
            hook(24 * q + 23, "dl", q, 1)
            hook(24 * q + 23, "dl", q, 2)
        for n_, name, *a in PLAN:
            hook(n_, name, *a)

        def unit(s, kind, *arg):
            if 0 <= s < NS:
                dict(tz=unit_tz, u=unit_u, tu=unit_tu, v=unit_v, xb=unit_xb, o=unit_o, rx=unit_rx,
                     xs=unit_xs, c=unit_c, ty=unit_ty, ys=unit_ys)[kind](s, *arg)
                if kind == "tz" and arg[0] == 1 and s + 1 < NS:
                    load_z(s + 1)
                if kind == "v" and s + 1 < NS:
                    load_ag(s + 1)
                if kind == "xb" and arg[0] == 1 and s + 1 < NS:
                    load_x(s + 1)

        unit(0, "tz", 0)
        unit(0, "tz", 1)
        load_ag(0)
        load_lora()
        for m in range(4):
            load_w(m)
        unit(0, "xb", 0)
        unit(0, "xb", 1)
        unit(0, "u", 0)
        unit(0, "u", 1)
        setup_a()
        unit(0, "tu")
        setup_cb()
        unit(0, "v")
        setup_taps()
        for i in range(4):
            unit(0, "o", i)
        setup_lora()
        unit(0, "rx", 0)
        unit(0, "rx", 1)
        unit(1, "tz", 0)
        unit(1, "tz", 1)
        sort_w(0)
        load_w(4)
        for m in range(4):
            sort_w(m + 1)
            if m < 3:
                load_w(m + 5)
            setup_w(m)
        unit(1, "xb", 0)
        unit(1, "xb", 1)
        unit(1, "u", 0)
        unit(1, "u", 1)
        unit(1, "tu")
        unit(0, "xs")
        setup_pad()
        for m in range(4, 8):
            if m < 7:
                sort_w(m + 1)
            setup_w(m)
        unit(1, "v")
        for g in range(4):
            unit(0, "c", g)
            unit(0, "ty", g)
        unit(0, "ys", 0)
        unit(0, "ys", 1)
        for i in range(4):
            unit(1, "o", i)
        unit(1, "rx", 0)
        unit(1, "rx", 1)
        for it in range(NS):
            for n_ in range(48):
                step_c(2 * it + n_ // 24, n_ % 24 // 8, n_ % 8)
                for name, a in hooks.get(n_, ()):
                    t = 2 * it + (a[0] if name not in "AB" else 0)
                    if name == "A":
                        unit(it + 2, *a)
                    elif name == "B":
                        unit(it + 1, *a)
                    elif name == "zc":
                        unit_zc(t)
                    elif name == "zt":
                        unit_zt(t)
                    else:
                        unit_dl(t, a[1])
                        unit_f(t, a[1])
        do("sp", lambda e: e.nop(), [("d_st", 16 * 2 * NS), d_agw, d_tap])

        block = ctx.enter_context(nc.Block())

        @block.sync
        def _(eng):
            play("sp", eng)

        @block.gpsimd
        def _(eng):
            play("pool", eng)

        @block.scalar
        def _(eng):
            play("act", eng)

        @block.vector
        def _(eng):
            play("dve", eng)

        @block.tensor
        def _(eng):
            play("pe", eng)


PLAN = [
    (2, "A", "tz", 0), (3, "A", "tz", 1), (7, "B", "xs"), (14, "A", "u", 0), (14, "A", "u", 1), (16, "A", "tu"),
    (18, "A", "v"), (20, "B", "c", 0), (23, "A", "xb", 0), (23, "A", "o", 0), (23, "B", "c", 1), (24, "B", "ty", 0),
    (24, "B", "ty", 1), (25, "A", "xb", 1), (27, "A", "o", 1), (27, "B", "c", 2), (31, "B", "c", 3),
    (33, "B", "ty", 2), (33, "B", "ty", 3), (38, "A", "o", 2), (38, "A", "o", 3), (39, "A", "rx", 0),
    (39, "B", "ys", 0), (42, "A", "rx", 1), (45, "B", "ys", 1),
]

_INS = ['x', 'cond_128', 'fside_S_0', 'L0_cond_W0', 'L0_cond_b0', 'L0_cond_W1', 'L0_cond_b1', 'L0_cond_W2', 'L0_cond_b2',
        'L0_cond_weight', 'L0_cond_bias_k', 'L0_ffn_A', 'L0_ffn_B', 'L0_ffn_bias', 'L1_cond_weight', 'L1_cond_c_weight',
        'L1_ffn_W_up', 'L1_ffn_gate_w', 'L1_ffn_expert_bias', 'L1_ffn_lora_A', 'L1_ffn_lora_B']


def kernel(**inputs):
    import numpy as _np
    import concourse.bacc as _bacc
    from concourse import mybir as _mybir
    from concourse.bass_utils import run_bass_kernel_spmd as _run

    nc = _bacc.Bacc("TRN2", target_bir_lowering=False, num_devices=1)
    arrays, args = {}, []
    for name in _INS:
        a = _np.ascontiguousarray(inputs[name])
        arrays[f"in_{name}_dram"] = a
        args.append(nc.dram_tensor(f"in_{name}_dram", a.shape, _mybir.dt.from_np(a.dtype), kind="ExternalInput").ap())
    o = nc.dram_tensor("out_0_dram", (NB, C, L), _mybir.dt.float32, kind="ExternalOutput").ap()
    adaln_ffn(nc, *args, o)
    r = _run(nc, [arrays], core_ids=[0])
    return r.results[0]["out_0_dram"]
```

```python
import concourse.bass as bass
from concourse import mybir
from contextlib import ExitStack

NB = 128
C = 64
L = 1024
RK = 128
E = 4
R = 8
NG = 4
NS = 32
WC = 36 + L
CH = [(0, 380), (380, 344), (724, 336)]
OFF = [36, 0, 0]
NA = [43, 43, 42]
A0 = [0, 43, 86]
XR = 5
YR = 3


def adaln_ffn(nc, x, cond, fside, W0, b0, W1, b1, W2, b2, wk, bias_k, A, B, fbias,
              cw, ccw, Wup, gate, ebias, loA, loB, out):
    fp32 = mybir.dt.float32
    f32r = mybir.dt.float32r
    ALU = mybir.AluOpType
    ACT = mybir.ActivationFunctionType
    AX = mybir.AxisListType

    x_v = x.rearrange("b c l -> (b c) l").rearrange("(s q p) l -> s p q l", q=2, p=128)
    z_v = x.rearrange("b c l -> (b c) l").rearrange("(s t i) l -> s i t l", t=8, i=32)
    out_v = out.rearrange("b c l -> (b c) l").rearrange("(t p) l -> t p l", p=128)
    aggD = nc.dram_tensor("agg_scratch", (NB, C, C), fp32, kind="Internal").ap()
    agbD = nc.dram_tensor("agb_scratch", (NB, C), fp32, kind="Internal").ap()
    tapT = nc.dram_tensor("tap_scratch", (16, C, 24), fp32, kind="Internal")
    tapD = tapT.ap()

    ctx = ExitStack()
    with ctx:
        place = {"": (nc.sbuf_base + 31) // 32 * 32}

        def sb(name, shape, dt=fp32):
            size = 4
            for n in shape[1:]:
                size *= n
            place[name] = place[""]
            place[""] += (size + 31) // 32 * 32
            assert place[""] <= nc.sbuf_usable_end
            return nc.alloc_sbuf_tensor_at(name, shape, dt, offset=place[name])

        def over(name, base, shape, start=0, dt=fp32):
            return nc.alloc_sbuf_tensor_at(name, shape, dt, offset=place[base] + 4 * start)

        Wh = sb("Wh", [128, 8, WC], f32r)
        Wl = sb("Wl", [128, 8, WC], f32r)
        Ah = sb("Ah", [128, 8, 128], f32r)
        Al = sb("Al", [128, 8, 128], f32r)
        Bh = sb("Bh", [128, 8, RK], f32r)
        Bl = sb("Bl", [128, 8, RK], f32r)
        Th = sb("Th", [128, NG, 2, 8, 16], f32r)
        Tl = sb("Tl", [128, NG, 2, 8, 16], f32r)
        Ls = sb("Ls", [96, L], f32r)
        biasb = sb("biasb", [128, L])
        ident = sb("ident", [128, 128])
        cb = sb("cb", [128, NB, NG])
        csB = sb("csB", [128, 1])
        ebb = sb("ebb", [128, E])
        wts = sb("wts", [128, E])
        xin = sb("xin", [128, 2, L])
        xTh = sb("xTh", [128, 8, 256], f32r)
        xTl = sb("xTl", [128, 8, 256], f32r)
        xTr = over("xTr", "xTl", [128, 8, 256])
        zin = sb("zin", [128, 8, 256])
        D = sb("D", [128, 2, 512])
        u = sb("u", [128, 256])
        agg = sb("agg", [128, 2, 128])
        agb = sb("agb", [128, 256])
        vh = sb("vh", [128, 256], f32r)
        vl = sb("vl", [128, 256], f32r)
        v = over("v", "vl", [128, 256])
        x1 = sb("x1", [128, XR, 8, 129])
        Xlo = sb("Xlo", [128, 4, NG, 129], f32r)
        Xhi = sb("Xhi", [128, 4, NG, 129], f32r)
        yh = sb("yh", [128, YR, 8, 128], f32r)
        yl = sb("yl", [128, YR, 8, 128], f32r)
        yr = over("yr", "yl", [128, YR, 8, 128])
        osb = sb("osb", [128, L])
        lg = sb("lg", [128, E])
        mx = sb("mx", [128, 1])
        sc = sb("sc", [128, E])
        m2 = sb("m2", [128, 1])
        zm = sb("zm", [128, E * R])
        zs = sb("zs", [128, 96])
        zst = sb("zst", [96, 128], f32r)

        O = [ctx.enter_context(nc.psum_tensor(f"O{i}", [128, 512], fp32)) for i in range(3)]
        F = [ctx.enter_context(nc.psum_tensor(f"F{i}", [128, 512], fp32)) for i in range(5)]

        queues = {e: [] for e in ("pe", "act", "dve", "pool", "sp")}
        sems, counts = {}, {}

        def do(engine, emit, after=(), sem=None, by=1):
            queues[engine].append((emit, [a for a in after if a], sem, by))
            if sem is None:
                return None
            if sem not in sems:
                sems[sem] = ctx.enter_context(nc.semaphore(sem))
                counts[sem] = 0
            counts[sem] += by
            return sem, counts[sem]

        def play(engine, eng):
            known = {}
            for emit, after, sem, by in queues[engine]:
                for name, value in after:
                    if known.get(name, 0) < value:
                        eng.wait_ge(sems[name], value)
                        known[name] = value
                ins = emit(eng)
                if sem is not None:
                    ins.then_inc(sems[sem], by)

        def load(dst, src, after=(), sem="d_set"):
            return do("sp", lambda e: e.dma_start(dst, src), after, sem, 16)

        def seq(*emits):
            def go(e):
                for f in emits:
                    last = f(e)
                return last
            return go

        T = {}
        evac = {}

        def g_(key):
            if key[1] < 0 or (key[0] == "u" and key[1] >= NS):
                return None
            return T[key]

        small = over("small", "Wl", [128, 1600], 4096)
        cnd = small[:, 0:128]
        W0s = small[:, 128:256]
        W1s = small[:, 256:384]
        W2s = small[:, 384:392]
        b2s = small[:, 392:400]
        b0s = small[:, 400:401]
        b1s = small[:, 401:402]
        fsr = small[0:1, 408:472]
        cwn = small[0:64, 512:640]
        bks = small[0:8, 640:704]
        condT = small[:, 768:896]
        h1 = small[:, 896:1024]
        h2 = small[:, 1024:1152]
        att = small[:, 1152:1160]
        atn = small[:, 1160:1168]
        nmx = small[:, 1168:1169]
        ssum = small[:, 1169:1170]
        rs = small[:, 1170:1171]
        attT = small[0:8, 1184:1312]
        ccT = small[:, 1312:1376]
        agbs = small[:, 1408:1472]
        ones = small[:, 1472:1600]
        aggS = over("aggS", "Wl", [128, C, C])
        wks = over("wks", "Wh", [24, 4096], 0, f32r)
        wk3 = over("wk3", "yh", [24, 4096])
        wkr = [over("wkr0", "Wl", [24, 2048], 5696, f32r), over("wkr1", "Th", [24, 2048], 0, f32r)]
        atsT = over("atsT", "Wl", [24, 128], 7744, f32r)
        ats = over("ats", "Wl", [128, 24], 7872)
        Bsum = over("Bsum", "Wl", [128, RK], 7904)
        low = over("low", "Wl", [24, 1], 8032)
        Uw = over("Uw", "Wh", [128, C, 24], 4096)
        taps = over("taps", "Wh", [64, 16, 24], 5632)
        cwX = over("cwX", "Wh", [128, NG, 8, 16], 6016)
        fsX = over("fsX", "Wh", [1, NG, 8, 16], 6528)
        Braw = over("Braw", "Xlo", [128, 8, RK])
        Araw = over("Araw", "Xlo", [128, 8, RK], 1024)
        LBr = over("LBr", "Xhi", [128, 8, E, R])
        LB3 = over("LB3", "Xhi", [128, 8, 3, E * R], 256)
        Graw = over("Graw", "Xhi", [36, L], 1024)
        ya, yb = over("ya", "yh", [128, YR, L]), over("yb", "yl", [128, YR, L])
        x1s = over("x1s", "x1", [128, L], 4 * 8 * 129)
        raw = [x1s[:, :], osb[:, :], ya[:, 1, :], yb[:, 1, :]]
        srt = [ya[:, 2, :], yb[:, 2, :], ya[:, 0, :], yb[:, 0, :]]

        T["tap0"] = do("pool", lambda e: e.memset(taps[:, :, :], 0.0), sem="g_id")
        T["id0"] = do("pool", lambda e: e.memset(ident[:, :], 0.0), sem="g_id")
        T["id"] = do("pool", lambda e: e.affine_select(out=ident[:, :], in_=ident[:, :], compare_op=ALU.not_equal,
                                                       fill=1.0, base=0, pattern=[[-1, 128]], channel_multiplier=1),
                     [T["id0"]], "g_id")
        T["low"] = do("pool", lambda e: e.memset(low[:, :], 1.0), sem="g_id")
        for i in range(E):
            do("pool", lambda e, i=i: e.memset(wts[:, i:i + 1], float(E - i)))
        do("pool", lambda e: e.memset(agg[:, :, :], 0.0))
        do("pool", lambda e: e.memset(x1[:, 0:4, 0:4, 0:1], 0.0))
        do("pool", lambda e: e.memset(x1[:, 0:4, 4:8, 128:129], 0.0))
        do("pool", lambda e: e.memset(ones, 1.0), sem="g_id")
        T["con"] = do("pool", lambda e: e.affine_select(out=low[:, :], in_=low[:, :], compare_op=ALU.is_ge, fill=0.0, base=-16,
                                                        pattern=[[0, 1]], channel_multiplier=1), [T["low"]], "g_id")

        def load_mlp():
            T["d_c"] = load(cnd, cond, sem="d_cnd")
            load(W0s, W0, sem="d_mlp")
            load(b0s, b0.rearrange("(p a) -> p a", a=1), sem="d_mlp")
            load(W1s, W1, sem="d_mlp")
            load(b1s, b1.rearrange("(p a) -> p a", a=1), sem="d_mlp")
            load(W2s, W2, sem="d_mlp")
            T["d_m"] = load(b2s, b2.rearrange("(a k) -> a k", a=1).broadcast_to([128, 8]), sem="d_mlp")

        def load_x(s):
            T["x", s] = do("sp", lambda e: e.dma_start(xin[:, :, :], x_v[s]), [g_(("xb", s - 1, 1))], "d_x", 16)

        def load_z(s):
            for a in range(4):
                T["z", s] = do("sp", lambda e, a=a: e.dma_start(zin[32 * a:32 * a + 32, :, :], z_v[s, :, :, 256 * a:256 * a + 256]),
                               [g_(("tz", s - 1, 1))], "d_z", 16)

        def load_b():
            for a in range(4):
                T["d_b"] = load(Braw[32 * a:32 * a + 32, :, :], B[256 * a:256 * a + 256, :].rearrange("(c i) k -> i c k", i=32), sem="d_b")

        def load_wk():
            for t in range(3):
                T["d_w3"] = load(wk3[8 * t:8 * t + 8, :], wk.rearrange("k o i a -> k (o i a)"), sem="d_w3")
            T["d_k"] = load(bks, bias_k, sem="d_wk")

        def load_taps():
            T["d_t"] = do("sp", lambda e: e.dma_start(taps[:, :, 8:17], cw), [T["tap0"]], "d_tap", 16)

        def store_taps():
            T["d_tw"] = do("sp", lambda e: e.dma_start(tapD.rearrange("i o m -> o i m"), taps[:, :, :]), [T["d_t"]], "d_tapw", 16)

        def load_windows():
            n = 24 * (C - 1) + 16
            src = bass.AP(tensor=tapT, offset=1, ap=[[24 * C, 16], [1, 8], [1, n]])
            T["d_u"] = load(Uw[:, :, :].rearrange("p o m -> p (o m)")[:, 0:n], src, [T["d_tw"]], "d_tapr")

        def load_a():
            T["d_a"] = load(Araw[:, :, :], A.rearrange("(j c) k -> j c k", c=8), sem="d_a")

        def load_bias():
            T["d_bi"] = load(biasb[:, :], fbias.rearrange("(a n) -> a n", a=1).broadcast_to([128, L]), sem="d_bi")

        def load_cc():
            load(cwn, ccw, sem="d_cc")
            T["d_cc"] = load(fsr, fside.rearrange("(a n) -> a n", a=1), sem="d_cc")

        def setup_mlp():
            pc = do("pe", lambda e: e.transpose(F[4][:, 0:128], cnd, ident[:, :]), [T["d_c"], T["id"]], "p_mlp")
            ac = T["condT"] = do("act", lambda e: e.activation(condT, F[4][:, 0:128], ACT.Copy), [pc], "a_mlp")
            p1 = do("pe", lambda e: e.matmul(F[4][:, 128:256], W0s, condT, start=True, stop=True), [ac, T["d_m"]], "p_mlp")
            a1 = do("act", lambda e: e.activation(h1, F[4][:, 128:256], ACT.Gelu, bias=b0s), [p1], "a_mlp")
            p2 = do("pe", lambda e: e.matmul(F[4][:, 256:384], W1s, h1, start=True, stop=True), [a1], "p_mlp")
            a2 = do("act", lambda e: e.activation(h2, F[4][:, 256:384], ACT.Gelu, bias=b1s), [p2], "a_mlp")
            p3 = do("pe", lambda e: e.matmul(F[4][:, 384:392], h2, W2s, start=True, stop=True), [a2], "p_mlp")
            w1 = do("dve", lambda e: e.tensor_tensor(att, F[4][:, 384:392], b2s, ALU.add), [p3, T["d_m"]], "v_mlp")
            w2 = do("dve", lambda e: e.tensor_reduce(nmx, att, AX.X, ALU.max, negate=True), [w1], "v_mlp")
            a3 = do("act", lambda e: e.activation(atn, att, ACT.Exp, bias=nmx, accum_out=ssum), [w2], "a_mlp")
            w3 = do("dve", lambda e: e.reciprocal(rs, ssum), [a3], "v_mlp")
            w4 = do("dve", lambda e: e.tensor_scalar(att, atn, rs, None, ALU.mult), [w3, a3], "v_mlp")
            p4 = do("pe", lambda e: e.transpose(F[3][0:8, 0:128], att, ident[:, :]), [w4], "p_mlp")
            w5 = do("dve", lambda e: e.tensor_copy(ats[:, 16:24].bitcast(f32r), att), [w4], "v_mlp")
            w6 = do("dve", lambda e: e.tensor_tensor(ats[:, 8:16].bitcast(f32r), ats[:, 16:24], att, ALU.subtract), [w5], "v_mlp")
            w6 = do("dve", lambda e: e.tensor_scalar(ats[:, 0:8].bitcast(f32r), ats[:, 16:24], -1.0, None, ALU.mult), [w6], "v_mlp")
            p5 = do("pe", lambda e: e.transpose(O[0][0:24, 0:128], ats[:, :], ident[:, :]), [w6], "p_mlp")
            T["attT"] = do("dve", lambda e: e.tensor_copy(attT, F[3][0:8, 0:128]), [p4], "v_mlp")
            T["atsT"] = do("dve", lambda e: e.tensor_copy(atsT[:, :], O[0][0:24, 0:128]), [p5], "v_mlp")

        def setup_wk(h):
            k_ = wk3[:, 2048 * h:2048 * h + 2048]
            r_ = do("act", lambda e: e.activation(wkr[h][:, :], k_, ACT.Copy), [T["d_w3"]], "a_wk")
            T["wk", h] = do("dve", lambda e: e.scalar_tensor_tensor(out=wks[:, 2048 * h:2048 * h + 2048], in0=k_, scalar=low[:, 0:1], in1=wkr[h][:, :].bitcast(fp32),
                                                                    op0=ALU.mult, op1=ALU.subtract), [r_, T["con"]], "v_wk")

        def setup_agg(c):
            bank = (O[0], O[1], O[2], F[0], F[1], F[2])[c % 6]
            pg = do("pe", lambda e: e.matmul(bank[:, :], atsT[:, :], wks[:, 512 * c:512 * c + 512],
                                                start=True, stop=True),
                    [T["atsT"], T["wk", c // 4], T["agc", c - 6] if c >= 6 else None], "p_ag")
            dst = aggS[:, :, 8 * c:8 * c + 8].rearrange("p i o -> p o i")
            src = bank[:, :].rearrange("p (o i) -> p o i", o=8)
            if c % 2:
                T["agc", c] = do("act", lambda e: e.activation(dst, src, ACT.Copy), [pg], "a_ag")
            else:
                T["agc", c] = do("dve", lambda e: e.tensor_copy(dst, src), [pg], "v_ag")
            if c == C // 8 - 1:
                for h, (b0_, b1_) in enumerate(((0, 8), (8, NB))):
                    T["aw", h] = do("sp", lambda e, b0_=b0_, b1_=b1_: e.dma_start(aggD[b0_:b1_], aggS[b0_:b1_]),
                                    [T["agc", c - 1], T["agc", c]], f"d_agw{h}", 16)

        def setup_agb():
            pb = do("pe", lambda e: e.matmul(F[4][:, 0:64], attT, bks, start=True, stop=True), [T["attT"], T["d_k"]], "p_ag")
            T["vb"] = do("dve", lambda e: e.tensor_copy(agbs, F[4][:, 0:64]), [pb], "v_ag")
            T["agw"] = do("sp", lambda e: e.dma_start(agbD, agbs), [T["vb"]], "d_agbw", 16)

        def setup_b():
            T["bh"] = do("act", lambda e: e.activation(Bh[:, :, :], Braw[:, :, :], ACT.Copy), [T["d_b"]], "a_b")
            T["bl"] = do("dve", lambda e: e.tensor_tensor(Bl[:, :, :], Braw[:, :, :], Bh[:, :, :].bitcast(fp32), ALU.subtract), [T["bh"]], "v_b")

        def setup_bsum():
            T["bsum"] = do("dve", lambda e: e.tensor_reduce(Bsum[:, :], Braw[:, :, :].rearrange("p c k -> p k c"), AX.X, ALU.add),
                           [T["d_b"]], "v_b")
            pcs = do("pe", lambda e: e.matmul(F[3][:, 0:1], Bsum[:, :], ones[:, 0:1], start=True, stop=True),
                     [T["bsum"], T["con"], T["atsT"], T["attT"]], "p_b")
            evac[3] = T["cs"] = do("dve", lambda e: e.tensor_copy(csB[:, :], F[3][:, 0:1]), [pcs], "v_b")

        def setup_a(h):
            pa = T["pa", h] = do("pe", seq(*[lambda e, c=c: e.transpose(F[h][:, 128 * c:128 * c + 128], Araw[:, 4 * h + c, :], ident[:, :])
                                             for c in range(4)]), [T["d_a"], T["agc", 3 + h]], "p_a")
            dh, dl = (t_[:, 4 * h:4 * h + 4, :].rearrange("p a b -> p (a b)") for t_ in (Ah, Al))
            ah = do("act", lambda e: e.activation(dh, F[h][:, :], ACT.Copy), [pa], "a_a")
            evac[h] = T["al", h] = do("dve", lambda e: e.tensor_tensor(dl, F[h][:, :], dh.bitcast(fp32), ALU.subtract), [ah], "v_a")

        def setup_taps():
            for blk in range(2):
                src = Uw[:, :, 8 * blk:8 * blk + 8].rearrange("p (g o) r -> p g r o", g=NG)[:, :, ::-1, :]
                for g in range(NG):
                    T["th", g, blk] = do("pool", lambda e, g=g, blk=blk, src=src: e.tensor_copy(Th[:, g, blk], src[:, g]),
                                          [T["d_u"], T["wk", 1]], "g_t")
            for blk in range(2):
                src = Uw[:, :, 8 * blk:8 * blk + 8].rearrange("p (g o) r -> p g r o", g=NG)[:, :, ::-1, :]
                for g in range(NG):
                    T["tl"] = do("pool", lambda e, g=g, blk=blk, src=src: e.tensor_tensor(
                        Tl[:, g, blk], src[:, g], Th[:, g, blk].bitcast(fp32), ALU.subtract), [T["th", g, blk]], "g_t")

        def setup_cb():
            pcc = do("pe", lambda e: e.transpose(F[2][:, 0:64], cwn, ident[0:64, 0:64]), [T["d_cc"], T["agc", 5]], "p_cb")
            acc = do("dve", lambda e: e.tensor_copy(ccT, F[2][:, 0:64]), [pcc], "v_cb")
            do("dve", lambda e: e.tensor_copy(fsX[:, :, :, :], fsr.rearrange("p (g o) -> p g o", g=NG).unsqueeze(2).broadcast_to([1, NG, 8, 16])),
               [T["d_cc"]], "v_cb")
            vx = do("dve", lambda e: e.tensor_copy(cwX[:, :, :, :], ccT.rearrange("p (g o) -> p g o", g=NG).unsqueeze(2).broadcast_to([128, NG, 8, 16])),
                    [acc], "v_cb")
            for g in range(NG):
                do("pe", lambda e, g=g: e.matmul(F[2][:, 128 * g:128 * g + 128], cwX[:, g].rearrange("p r o -> p (r o)"), condT,
                                                 start=True, stop=False), [vx, T["condT"], T["con"]])
                T["pcb"] = do("pe", lambda e, g=g: e.matmul(F[2][:, 128 * g:128 * g + 128], fsX[:, g].rearrange("p r o -> p (r o)"), ones[0:1, :],
                                                            start=False, stop=True), (), "p_cb")
            evac[2] = T["cb"] = do("dve", lambda e: e.tensor_copy(cb[:, :, :].rearrange("p b g -> p g b"),
                                                                  F[2][:, :].rearrange("p (g b) -> p g b", g=NG)), [T["pcb"]], "v_cb")

        def sorted_copy(dst, src, after, sem):
            for r in range(2):
                d_ = dst.rearrange("p (b r q i) -> p b r q i", b=4, r=2, q=4)[:, :, r]
                s_ = src.rearrange("p (b i q r) -> p b r q i", b=4, i=32, q=4)[:, :, r]
                t_ = do("act", lambda e, d_=d_, s_=s_: e.activation(d_, s_, ACT.Copy), after, sem)
            return t_

        def load_lora():
            do("sp", lambda e: e.dma_start(ebb[:, :], ebias.rearrange("(a n) -> a n", a=1).broadcast_to([128, E])), (), "d_lo", 16)
            do("sp", lambda e: e.dma_start(Graw[0:4, :], gate), (), "d_lo", 16)
            do("sp", lambda e: e.dma_start(Graw[4:36, :], loA.rearrange("e r h -> (e r) h")), (), "d_lo", 16)
            for e_ in range(E):
                T["lo"] = load(LBr[:, :, e_, :], loB[e_].rearrange("(m p) r -> p m r", p=128), sem="d_lo")

        def setup_lb():
            LB2 = LBr[:, :, :, :].rearrange("p m e r -> p m (e r)")
            for t in range(2):
                l_h = do("dve", lambda e, t=t: e.tensor_copy(LB3[:, :, t, :].bitcast(f32r), LB2), [T["lo"]], "v_lo")
            l_l = do("dve", lambda e: e.tensor_tensor(LB3[:, :, 2, :].bitcast(f32r), LB2, LB3[:, :, 0, :], ALU.subtract), [l_h], "v_lo")
            for h in range(2):
                pl = do("pe", seq(*[lambda e, h=h, m=m: e.transpose(O[h][0:96, 128 * m:128 * m + 128],
                                                                   LB3[:, 4 * h + m].rearrange("p t n -> p (t n)"), ident[:, :])
                                    for m in range(4)]), [l_l, T["agc", 7], T["agc", 6]], "p_lo")
                T["ls"] = do("act", lambda e, h=h: e.activation(Ls[:, 512 * h:512 * h + 512], O[h][0:96, :], ACT.Copy), [pl], "a_lo")

        def setup_g():
            gs = sorted_copy(ya[0:36, 2, :], Graw[:, :], [T["lo"], T["wk", 1]], "a_lo")
            pg = T["pg"] = do("pe", seq(*[lambda e, c=c: e.transpose(O[2][:, 36 * c:36 * c + 36], ya[0:36, 2, 128 * c:128 * c + 128], ident[0:36, 0:36])
                                          for c in range(8)]), [gs, T["agc", 2]], "p_lo")
            src = O[2][:, 0:288].rearrange("p (c n) -> p c n", c=8)
            T["small"] = [T["aw", 0], T["aw", 1], T["agw"], T["tl"], T["pcb"], T["cb"], T["cs"], T["d_tw"]]
            gh = do("act", lambda e: e.activation(Wh[:, :, 0:36], src, ACT.Copy), [pg] + T["small"], "a_lo")
            T["g"] = do("dve", lambda e: e.tensor_tensor(Wl[:, :, 0:36], src, Wh[:, :, 0:36].bitcast(fp32), ALU.subtract), [gh], "v_lo")

        def load_w(m):
            T["wl", m] = load(raw[(m + 2) % 4], Wup[128 * m:128 * m + 128, :], [T["ws", m - 4] if m > 3 else T["wk", 1]], f"d_w{m % 4}")

        def sort_w(m):
            T["ws", m] = sorted_copy(srt[(m + 2) % 4], raw[(m + 2) % 4], [T["wl", m], T["pw", m - 4] if m > 3 else T["pg"]], "a_ws")

        def setup_w(m):
            for h in range(2):
                half_w(m, h, (2 * m + h) % 3 if m < 3 else 1 + h)

        def half_w(m, h, i):
            n = 2 * m + h
            bank, before = O[i], T["wb", i] if n > 2 else None
            T["pw", m] = do("pe", seq(*[lambda e, c=c: e.transpose(
                bank[:, 128 * c:128 * c + 128], srt[(m + 2) % 4][:, 512 * h + 128 * c:512 * h + 128 * c + 128], ident[:, :])
                for c in range(4)]), [T["ws", m], before, T["g"], T["ls"]], "p_w")
            dh, dl = (t_[:, 4 * h:4 * h + 4, 36 + 128 * m:164 + 128 * m] for t_ in (Wh, Wl))
            src = bank[:, :].rearrange("p (c n) -> p c n", c=4)
            aw = do("act", lambda e: e.activation(dh, src, ACT.Copy), [T["pw", m]] + T["small"], "a_w")
            T["w", n] = T["wb", i] = do("dve", lambda e: e.tensor_tensor(dl, src, dh.bitcast(fp32), ALU.subtract), [aw], "v_w")

        def setup_pad():
            do("pool", lambda e: e.memset(x1[:, 4, 0:4, 0:1], 0.0), [T["ws", 6]])
            T["pad"] = do("pool", lambda e: e.memset(x1[:, 4, 4:8, 128:129], 0.0), [T["ws", 6]], "g_pad")

        def load_ag(s):
            prev = [g_(("v", s - 1)), g_(("vv", s - 1)), T["aw", int(s > 1)], T["agw"], T["con"]]
            for b in range(2):
                src = aggD[4 * s + b:4 * s + b + 3:2].rearrange("q c o -> c q o")
                do("sp", lambda e, b=b, src=src: e.dma_start(agg[64 * b:64 * b + 64, :, 64 * b:64 * b + 64], src), prev, "d_ag", 16)
            src = agbD[4 * s:4 * s + 4, :].rearrange("(a b) o -> a (b o)", a=1).broadcast_to([128, 256])
            T["ag", s] = do("sp", lambda e: e.dma_start(agb[:, :], src), prev, "d_ag", 16)

        def unit_tz(s, q):
            src = zin[:, 4 * q:4 * q + 4, :].rearrange("p t (k i) -> p t k i", i=32)
            dst = xTr[:, :, 128 * q:128 * q + 128].rearrange("p k (t i) -> p t k i", i=32)
            T["tz", s, q] = do("dve", lambda e: e.transpose(dst, src), [T["z", s], g_(("u", s - 1)), g_(("txl", s - 1, q))], "v_tz")
            dh, dl, dr = (t_[:, :, 128 * q:128 * q + 128] for t_ in (xTh, xTl, xTr))
            T["txh", s, q] = do("act", lambda e: e.activation(dh, dr, ACT.Copy), [T["tz", s, q], g_(("u", s - 1))], "a_txh")
            T["txl", s, q] = do("pool", lambda e: e.tensor_tensor(dl, dr, dh.bitcast(fp32), ALU.subtract), [T["txh", s, q]], "g_txl")

        def unit_u(s, half):
            ms = []
            for c in range(4 * half, 4 * half + 4):
                for n_, (w, m) in enumerate(((Bh, xTh), (Bh, xTl), (Bl, xTh))):
                    ms.append(lambda e, c=c, w=w, m=m, n_=n_: e.matmul(F[4][:, 0:256], w[:, c, :], m[:, c, :],
                                                                      start=c == 0 and n_ == 0, stop=c == 7 and n_ == 2))
            T["u", s] = do("pe", seq(*ms), [T["txl", s, 0], T["txl", s, 1], g_(("vv", s - 1)), T["bl"], T["vb"]], "p_u")
            if half:
                T["ut", s] = do("act", lambda e: e.activation(u[:, :], F[4][:, 0:256], ACT.Copy), [T["u", s], g_(("v", s - 1))], "a_u")

        def unit_tu(s):
            T["tu", s] = do("pe", seq(*[lambda e, q=q: e.transpose(F[4][:, 128 * q:128 * q + 128], u[:, 128 * q:128 * q + 128], ident[:, :])
                                        for q in range(2)]), [T["ut", s]], "p_tu")
            T["tuu", s] = do("act", lambda e: e.activation(u[:, :], F[4][:, 0:256], ACT.Copy), [T["tu", s]], "a_tu")

        def unit_v(s):
            T["v", s] = do("pe", seq(*[lambda e, q=q: e.matmul(F[4][:, 128 * q:128 * q + 128], u[:, 128 * q:128 * q + 128], agg[:, q, :],
                                                               start=True, stop=True) for q in range(2)]),
                           [T["tuu", s], T["ag", s]], "p_v")
            T["vv", s] = do("dve", lambda e: e.scalar_tensor_tensor(out=v[:, :], in0=agb[:, :], scalar=csB[:, 0:1], in1=F[4][:, 0:256],
                                                                    op0=ALU.mult, op1=ALU.add),
                            [T["v", s], T["ag", s], g_(("vh", s - 1)), T["cs"], g_(("vl", s - 1)), g_(("o", s - 1, 3))], "v_v")
            T["vh", s] = do("act", lambda e: e.activation(vh[:, :], v[:, :], ACT.Copy), [T["vv", s], g_(("o", s - 1, 3))], "a_vh")
            T["vl", s] = do("dve", lambda e: e.tensor_tensor(vl[:, :], v[:, :], vh[:, :].bitcast(fp32), ALU.subtract),
                            [T["vh", s], g_(("o", s - 1, 3))], "v_vl")

        def slot(s, q):
            return (2 * s + q) % XR

        def unit_xb(s, q):
            t = 2 * s + q
            xs = xin[:, q, :].rearrange("p (a c) -> p c a", c=8)
            bs = biasb[:, :].rearrange("p (a c) -> p c a", c=8)
            o = x1[:, slot(s, q)]
            for h in range(2):
                dst = o[:, 4:8, 0:128] if h == 0 else o[:, 0:4, 1:129]
                T["xb", s, q] = do("pool", lambda e, h=h, dst=dst: e.tensor_tensor(dst, xs[:, 4 * h:4 * h + 4, :], bs[:, 4 * h:4 * h + 4, :], ALU.add),
                                   [T["x", s], g_(("f", t - XR, 2)), g_(("rx", (t - XR) // 2, (t - XR) % 2)), T["d_bi"], T["con"], T["pad"] if t == 4 else None], "g_xb")

        def unit_o(s, i):
            q, h = i // 2, i % 2
            ms = []
            for n_, (w, m) in enumerate(((vh, Ah), (vh, Al), (vl, Ah))):
                ms.append(lambda e, w=w, m=m, n_=n_: e.matmul(F[i][:, :], w[:, 128 * q:128 * q + 128],
                                                             m[:, 4 * h:4 * h + 4, :].rearrange("p c a -> p (c a)"),
                                                             start=n_ == 0, stop=n_ == 2))
            T["o", s, i] = do("pe", seq(*ms), [T["vl", s], T["al", 1], evac[i]], "p_o")
            o = x1[:, slot(s, q)]
            dst = o[:, 4:8, 0:128] if h == 0 else o[:, 0:4, 1:129]
            evac[i] = T["x1", s, i] = do("dve", lambda e: e.tensor_tensor(dst, F[i][:, :].rearrange("p (c a) -> p c a", c=4), dst, ALU.add),
                               [T["o", s, i], T["xb", s, q]], "v_x1")

        def unit_rx(s, q):
            for b in range(2):
                for g in range(NG):
                    p0 = 64 * b + 16 * g
                    T["rx", s, q] = do("sp", lambda e, b=b, g=g, p0=p0: e.dma_start(
                        Xlo[:, 2 * q + b, g, :].bitcast(fp32), x1[p0:p0 + 16, slot(s, q), :, :]),
                        [T["x1", s, 2 * q], T["x1", s, 2 * q + 1], g_(("c", s - 1, 3)), T["bl"], T["bsum"], T["pa", 1]], "d_rx", 16)

        def unit_xs(s):
            T["xs1", s] = do("act", lambda e: e.activation(Xhi[:, :, :, :], Xlo[:, :, :, :].bitcast(fp32), ACT.Copy),
                             [T["rx", s, 1], g_(("c", s - 1, 3)), T["pg"]], "a_xs")
            T["xs", s] = do("dve", lambda e: e.tensor_tensor(Xlo[:, :, :, :], Xlo[:, :, :, :].bitcast(fp32),
                                                            Xhi[:, :, :, :].bitcast(fp32), ALU.subtract), [T["xs1", s]], "v_xs")

        def unit_c(s, g):
            ms = []
            for blk in range(2):
                for n_, (w, m) in enumerate(((Th, Xhi), (Tl, Xhi), (Th, Xlo))):
                    ms.append(lambda e, w=w, m=m, blk=blk, n_=n_: e.matmul(
                        F[g][:, :], w[:, g, blk].rearrange("p r o -> p (r o)"), m[:, :, g, blk:blk + 128],
                        start=blk == 0 and n_ == 0, stop=blk == 1 and n_ == 2))
            T["c", s, g] = do("pe", seq(*ms), [T["xs", s], T["tl"], evac[g]], "p_c")
            evac[g] = T["dd", s, g] = do("dve", lambda e: e.tensor_tensor(
                D[:, g % 2, :].rearrange("p (b j) -> p b j", b=4), F[g][:, :].rearrange("p (b j) -> p b j", b=4),
                cb[:, 4 * s:4 * s + 4, g].unsqueeze(2).broadcast_to([128, 4, 128]), ALU.add),
                [T["c", s, g], T["ty", s, g - 2, 1] if g > 1 else g_(("ty", s - 1, g + 2, 1)), T["cb"]], "v_d")

        def unit_ty(s, g):
            for q in range(2):
                src = D[:, g % 2, 256 * q:256 * q + 256].rearrange("p (b i) -> p b i", i=32)
                dst = yr[:, (2 * s + q) % YR].rearrange("p (k r) (b n) -> p b k r n", r=2, b=2)[:, :, :, :, 16 * g:16 * g + 16]
                pt = 2 * s + q - YR
                T["ty", s, g, q] = do("dve", lambda e, dst=dst, src=src: e.transpose(dst, src),
                                      [T["dd", s, g], g_(("cc", pt, 2)), T["pw", 5 if s == 0 else 7]], "v_ty")

        def unit_ys(s, q):
            ys = (2 * s + q) % YR
            T["yh", s, q] = do("act", lambda e: e.activation(yh[:, ys], yr[:, ys], ACT.Copy),
                               [T["ty", s, 3, q], g_(("cc", 2 * s + q - YR, 2)), T["pw", 5 if s == 0 else 7]], "a_yh")
            T["yl", s, q] = do("dve", lambda e: e.tensor_tensor(yl[:, ys], yr[:, ys], yh[:, ys].bitcast(fp32), ALU.subtract),
                               [T["yh", s, q]], "v_yl")

        def step_c(t, c, k):
            ys = t % YR
            c0, w_ = CH[c]
            ms = []
            for n_, (w, m) in enumerate(((yh, Wh), (yh, Wl), (yl, Wh))):
                ms.append(lambda e, w=w, m=m, n_=n_: e.matmul(O[c][:, 0:w_], w[:, ys, k, :], m[:, k, c0:c0 + w_],
                                                             start=k == 0 and n_ == 0, stop=k == 7 and n_ == 2))
            done = do("pe", seq(*ms), [T["yl", t // 2, t % 2], g_(("f", t - 1, c)), T["w", (5, 14, 15)[c]],
                                       g_(("zst", t)) if c == 2 else None], "p_cc")
            if k == 7:
                T["cc", t, c] = done

        def unit_zc(t):
            z = O[0][:, 4:36].rearrange("p (e r) -> p e r", e=E)
            a = do("dve", lambda e: e.tensor_tensor(lg[:, :], O[0][:, 0:4], ebb[:, :], ALU.add), [T["cc", t, 0], T["lo"]], "v_z")
            a = do("dve", lambda e: e.reduce_max(mx[:, :], lg[:, :], AX.X), [a], "v_z")
            a = do("dve", lambda e: e.scalar_tensor_tensor(out=sc[:, :], in0=lg[:, :], scalar=mx[:, 0:1], in1=wts[:, :],
                                                           op0=ALU.is_equal, op1=ALU.mult), [a, T["con"]], "v_z")
            a = do("dve", lambda e: e.reduce_max(m2[:, :], sc[:, :], AX.X), [a], "v_z")
            a = do("dve", lambda e: e.scalar_tensor_tensor(
                out=zm[:, :].rearrange("p (e r) -> p e r", e=E), in0=sc[:, :].unsqueeze(2).broadcast_to([128, E, R]),
                scalar=m2[:, 0:1], in1=z, op0=ALU.is_equal, op1=ALU.mult), [a], "v_z")
            zz = zs[:, :].rearrange("p (t n) -> p t n", t=3)
            a = do("dve", lambda e: e.tensor_copy(zz[:, 0::2, :].bitcast(f32r), zm[:, :].unsqueeze(1).broadcast_to([128, 2, 32])),
                   [a, g_(("zt", t - 1))], "v_z")
            T["zc", t] = do("dve", lambda e: e.tensor_tensor(zz[:, 1, :].bitcast(f32r), zm[:, :], zz[:, 0, :], ALU.subtract), [a], "v_z")

        def unit_zt(t):
            T["zt", t] = do("pe", lambda e: e.transpose(O[2][0:96, 0:128], zs[:, :], ident[:, :]), [T["zc", t], g_(("f", t - 1, 2))], "p_zt")
            T["zst", t] = do("act", lambda e: e.activation(zst[:, :], O[2][0:96, 0:128], ACT.Copy), [T["zt", t], g_(("dl", t - 1, 2))], "a_zt")

        def unit_dl(t, c):
            n0, w_ = 8 * A0[c], 8 * NA[c]
            T["dl", t, c] = do("pe", lambda e: e.matmul(O[c][:, OFF[c]:OFF[c] + w_], zst[:, :], Ls[:, n0:n0 + w_], start=False, stop=True,
                                                        skip_group_check=True), [T["zst", t], T["ls"]], "p_dl")

        def unit_f(t, c):
            n0, na = 8 * A0[c], NA[c]
            src = O[c][:, OFF[c]:OFF[c] + 8 * na].rearrange("p (a c) -> p a c", c=8)
            dst = osb[:, n0:n0 + 8 * na].rearrange("p (a c) -> p a c", c=8)
            xs = x1[:, t % XR].rearrange("p r j -> p j r")
            do("dve", lambda e: e.tensor_tensor(dst[:, :, 0:4], src[:, :, 0:4], xs[:, A0[c]:A0[c] + na, 4:8], ALU.add),
               [T["dl", t, c], g_(("st", t - 1)), T["x1", t // 2, 2 * (t % 2) + 1]])
            T["f", t, c] = do("dve", lambda e: e.tensor_tensor(dst[:, :, 4:8], src[:, :, 4:8], xs[:, A0[c] + 1:A0[c] + 1 + na, 0:4], ALU.add),
                              (), "v_f")
            if c == 2:
                T["st", t] = do("sp", lambda e: e.dma_start(out_v[t], osb[:, :]), [T["f", t, 2]], "d_st", 16)

        hooks = {}

        def hook(n_, fn, *a):
            hooks.setdefault(n_, []).append((fn, a))

        for q in range(2):
            hook(24 * q + 7, "zc", q)
            hook(24 * q + 14, "zt", q)
            hook(24 * q + 17, "dl", q, 0)
            hook(24 * q + 23, "dl", q, 1)
            hook(24 * q + 23, "dl", q, 2)
        for n_, name, *a in PLAN:
            hook(n_, name, *a)

        def unit(s, kind, *arg):
            if 0 <= s < NS:
                dict(tz=unit_tz, u=unit_u, tu=unit_tu, v=unit_v, xb=unit_xb, o=unit_o, rx=unit_rx,
                     xs=unit_xs, c=unit_c, ty=unit_ty, ys=unit_ys)[kind](s, *arg)
                if kind == "tz" and arg[0] == 1 and s + 1 < NS:
                    load_z(s + 1)
                if kind == "v" and s + 1 < NS:
                    load_ag(s + 1)
                if kind == "xb" and arg[0] == 1 and s + 1 < NS:
                    load_x(s + 1)

        parts = dict(load_mlp=load_mlp, load_x=load_x, load_z=load_z, load_b=load_b, load_wk=load_wk, load_taps=load_taps,
                     store_taps=store_taps, load_windows=load_windows, load_a=load_a, load_bias=load_bias, load_cc=load_cc,
                     mlp=setup_mlp, agg=setup_agg, agb=setup_agb, b=setup_b, wk=setup_wk, bsum=setup_bsum, a=setup_a, taps=setup_taps,
                     cb=setup_cb, load_lora=load_lora, lb=setup_lb, g=setup_g, load_w=load_w, sort_w=sort_w, w=setup_w,
                     pad=setup_pad, load_ag=load_ag)
        def part(name, *arg):
            if isinstance(name, int):
                unit(name, *arg)
            else:
                parts[name](*arg)

        go = START.index(("go",))
        for p in START[:go]:
            part(*p)
        for it in range(NS):
            for n_ in range(48):
                step_c(2 * it + n_ // 24, n_ % 24 // 8, n_ % 8)
                if it == 0:
                    for p in START[go + 1 + 2 * n_:go + 3 + 2 * n_]:
                        part(*p)
                for name, a in hooks.get(n_, ()):
                    t = 2 * it + (a[0] if name not in "ZAB" else 0)
                    if name == "A":
                        unit(it + 2, *a)
                    elif name == "Z":
                        unit(it + 3, *a)
                    elif name == "B":
                        unit(it + 1, *a)
                    elif name == "zc":
                        unit_zc(t)
                    elif name == "zt":
                        unit_zt(t)
                    else:
                        unit_dl(t, a[1])
                        unit_f(t, a[1])
        do("sp", lambda e: e.nop(), [("d_st", 16 * 2 * NS), T["aw", 0], T["aw", 1], T["agw"], T["d_tw"]])

        block = ctx.enter_context(nc.Block())

        @block.sync
        def _(eng):
            play("sp", eng)

        @block.gpsimd
        def _(eng):
            play("pool", eng)

        @block.scalar
        def _(eng):
            play("act", eng)

        @block.vector
        def _(eng):
            play("dve", eng)

        @block.tensor
        def _(eng):
            play("pe", eng)


PLAN = [
    (10, "B", "xs"), (11, "A", "xb", 0), (12, "A", "u", 0), (12, "A", "u", 1), (15, "A", "tu"), (17, "A", "v"),
    (19, "B", "c", 0), (21, "B", "c", 1), (23, "B", "ty", 0), (24, "B", "c", 2), (24, "A", "o", 0),
    (25, "B", "ty", 1), (25, "A", "xb", 1), (27, "A", "o", 1), (28, "B", "c", 3), (28, "B", "ty", 2),
    (29, "Z", "tz", 0), (31, "B", "ty", 3), (37, "B", "ys", 0), (37, "A", "o", 2), (39, "A", "o", 3),
    (39, "A", "rx", 0), (43, "B", "ys", 1), (45, "A", "rx", 1), (47, "Z", "tz", 1),
]

START = [
    ("load_mlp",), ("load_a",), ("mlp",), ("load_taps",), ("load_wk",), ("load_z", 0), ("store_taps",), ("load_b",),
    ("wk", 0), ("load_x", 0), ("load_lora",), ("load_windows",), (0, "tz", 0), (0, "tz", 1), ("agb",), ("agg", 0),
    ("wk", 1), ("agg", 1), ("b",), ("agg", 2), ("agg", 3), ("a", 0), ("load_w", 0), ("agg", 4), ("agg", 5),
    ("load_bias",), ("taps",), ("load_cc",), ("agg", 6), ("agg", 7), ("load_ag", 0), ("load_w", 1), ("load_w", 2),
    (0, "xb", 0), (0, "u", 0), ("bsum",), (0, "u", 1), ("lb",), (1, "tz", 0), ("cb",), ("g",), (0, "tu"), ("a", 1),
    ("sort_w", 0), ("load_w", 3), (0, "v"), (0, "o", 0), ("load_w", 4), ("sort_w", 1), (0, "o", 1), ("w", 0),
    ("sort_w", 2), (0, "xb", 1), (0, "rx", 0), (1, "tz", 1), ("w", 1), (0, "o", 2), ("sort_w", 3), (0, "o", 3),
    ("w", 2), (0, "rx", 1), ("load_w", 5), ("sort_w", 4), ("w", 3), ("w", 4), (0, "xs"), ("load_w", 6), (1, "u", 0),
    (1, "u", 1), (1, "tu"), (1, "xb", 0), ("sort_w", 5), (1, "xb", 1), (1, "v"), ("load_w", 7), ("w", 5), (0, "c", 0),
    (2, "tz", 0), (0, "ty", 0), (0, "c", 1), (1, "o", 0), (0, "ty", 1), ("sort_w", 6), (0, "c", 2), (1, "o", 1),
    (0, "c", 3), (0, "ty", 2), (0, "ty", 3), ("w", 6), ("sort_w", 7), (1, "o", 2), (1, "rx", 0), (0, "ys", 0),
    (1, "o", 3), (1, "rx", 1), (2, "tz", 1), ("w", 7), (0, "ys", 1), ("pad",), ("go",),
]

_INS = ['x', 'cond_128', 'fside_S_0', 'L0_cond_W0', 'L0_cond_b0', 'L0_cond_W1', 'L0_cond_b1', 'L0_cond_W2', 'L0_cond_b2',
        'L0_cond_weight', 'L0_cond_bias_k', 'L0_ffn_A', 'L0_ffn_B', 'L0_ffn_bias', 'L1_cond_weight', 'L1_cond_c_weight',
        'L1_ffn_W_up', 'L1_ffn_gate_w', 'L1_ffn_expert_bias', 'L1_ffn_lora_A', 'L1_ffn_lora_B']


def kernel(**inputs):
    import numpy as _np
    import concourse.bacc as _bacc
    from concourse import mybir as _mybir
    from concourse.bass_utils import run_bass_kernel_spmd as _run

    nc = _bacc.Bacc("TRN2", target_bir_lowering=False, num_devices=1)
    arrays, args = {}, []
    for name in _INS:
        a = _np.ascontiguousarray(inputs[name])
        arrays[f"in_{name}_dram"] = a
        args.append(nc.dram_tensor(f"in_{name}_dram", a.shape, _mybir.dt.from_np(a.dtype), kind="ExternalInput").ap())
    o = nc.dram_tensor("out_0_dram", (NB, C, L), _mybir.dt.float32, kind="ExternalOutput").ap()
    adaln_ffn(nc, *args, o)
    r = _run(nc, [arrays], core_ids=[0])
    return r.results[0]["out_0_dram"]
```
